# Optimizing a Trainium2 kernel written in Bass

```python
import numpy as np
import jax
import jax.numpy as jnp

def _softmax(x, axis=-1):
    return jax.nn.softmax(x, axis=axis)
def _gelu(x):
    return jax.nn.gelu(x, approximate=True)
def _silu(x):
    return jax.nn.silu(x)
def _sigmoid(x):
    return jax.nn.sigmoid(x)
def _layernorm(x, axis=-1, eps=1e-5):
    m = jnp.mean(x, axis=axis, keepdims=True)
    v = jnp.var(x, axis=axis, keepdims=True)
    return (x - m) / jnp.sqrt(v + eps)
def _scatter_add(tgt, idx, src, axis=0):
    return tgt.at[idx].add(src)
def _segment_sum(src, seg, n):
    return jax.ops.segment_sum(src, seg, n)

kernel_name = 'mk_adj_resnorm_d2_adj_128_3ebd18'

def setup_inputs(seed: int = 0):
    np.random.seed(seed)
    _w = jnp.asarray
    def _rec_inputs():
        import jax
        import jax.numpy as jnp
        _gk = jax.random.key(seed)
        x = -0.0003972 + 0.9999 * jax.random.normal(jax.random.fold_in(_gk, 1), (8, 2048, 128), jnp.float32)
        _a = jax.random.bernoulli(jax.random.fold_in(_gk, 2), 0.00195312, (8, 2048, 2048))
        _a = jnp.logical_or(_a, jnp.swapaxes(_a, -1, -2))
        _a = jnp.logical_or(_a, jnp.eye(2048, dtype=bool))
        adj = _a.astype(jnp.int32)
        return x, adj
    x, adj = _rec_inputs()
    def _L0_gnn_setup():
        import jax, jax.numpy as jnp
        import numpy as np
        LEAKY_ALPHA = 0.2
        NEG_INF = -9000000000000000.0
        key = jax.random.key(seed)
        ks = jax.random.split(key, 6)
        B, N, D = (512, 200, 128)
        h = jax.random.normal(ks[0], (B, N, D), dtype=jnp.float32)
        adj = jax.random.randint(ks[1], (B, N, N), 0, 5, dtype=jnp.int32)
        a_0 = jax.random.normal(ks[2], (D,), dtype=jnp.float32)
        a_1 = jax.random.normal(ks[3], (D,), dtype=jnp.float32)
        a_2 = jax.random.normal(ks[4], (D,), dtype=jnp.float32)
        a_3 = jax.random.normal(ks[5], (D,), dtype=jnp.float32)
        return {'h': h, 'adj': adj, 'a_0': a_0, 'a_1': a_1, 'a_2': a_2, 'a_3': a_3}
    _L0_gnn_all = _L0_gnn_setup()
    _L0_gnn_in = {k: v for k, v in _L0_gnn_all.items() if k in ('a_0', 'a_1', 'a_2', 'a_3', )}
    del _L0_gnn_all

    def _L1_gnn_setup():
        import jax, jax.numpy as jnp
        import numpy as np
        E = 128
        H = 4
        D = E // H
        NEG = -1000000000.0
        key = jax.random.key(seed)
        ks = jax.random.split(key, 4)
        B, N = (8, 2048)
        x = jax.random.normal(ks[0], (B, N, E), dtype=jnp.float32)
        adj = jax.random.randint(ks[1], (B, N, N), 0, 2, dtype=jnp.int32)
        in_proj_w = jax.random.normal(ks[2], (3 * E, E), dtype=jnp.float32) * (1.0 / np.sqrt(E))
        in_proj_b = jnp.zeros((3 * E,), dtype=jnp.float32)
        out_w = jax.random.normal(ks[3], (E, E), dtype=jnp.float32) * (1.0 / np.sqrt(E))
        out_b = jnp.zeros((E,), dtype=jnp.float32)
        return {'x': x, 'adj': adj, 'in_proj_w': in_proj_w, 'in_proj_b': in_proj_b, 'out_w': out_w, 'out_b': out_b}
    _L1_gnn_all = _L1_gnn_setup()
    _L1_gnn_in = {k: v for k, v in _L1_gnn_all.items() if k in ('in_proj_w', 'in_proj_b', 'out_w', 'out_b', )}
    del _L1_gnn_all

    return {
        "x": x,
        "adj": adj,
        "L0_gnn_a_0": _L0_gnn_in["a_0"],
        "L0_gnn_a_1": _L0_gnn_in["a_1"],
        "L0_gnn_a_2": _L0_gnn_in["a_2"],
        "L0_gnn_a_3": _L0_gnn_in["a_3"],
        "L1_gnn_in_proj_w": _L1_gnn_in["in_proj_w"],
        "L1_gnn_in_proj_b": _L1_gnn_in["in_proj_b"],
        "L1_gnn_out_w": _L1_gnn_in["out_w"],
        "L1_gnn_out_b": _L1_gnn_in["out_b"],
    }

def reference(x, adj, L0_gnn_a_0, L0_gnn_a_1, L0_gnn_a_2, L0_gnn_a_3, L1_gnn_in_proj_w, L1_gnn_in_proj_b, L1_gnn_out_w, L1_gnn_out_b):
    import jax
    import jax.numpy as jnp
    def _L0_gnn_ref(h, adj, a_0, a_1, a_2, a_3):
        import jax, jax.numpy as jnp
        import numpy as np
        LEAKY_ALPHA = 0.2
        NEG_INF = -9000000000000000.0
        def scores(a):
            return jax.nn.leaky_relu(jnp.einsum('bnd,bmd->bnm', h * a, h), negative_slope=LEAKY_ALPHA)
        alpha = jnp.full(adj.shape, jnp.float32(NEG_INF), dtype=h.dtype)
        for k, a in enumerate((a_0, a_1, a_2, a_3)):
            alpha = jnp.where(adj == k + 1, scores(a), alpha)
        alpha = jax.nn.softmax(alpha, axis=-1)
        return jnp.einsum('bnm,bmd->bnd', alpha, h)

    def _L1_gnn_ref(x, adj, in_proj_w, in_proj_b, out_w, out_b):
        import jax, jax.numpy as jnp
        import numpy as np
        E = 128
        H = 4
        D = E // H
        NEG = -1000000000.0
        B, N, _ = x.shape
        mask = jnp.where(adj[0] == 0, jnp.float32(NEG), jnp.float32(0.0))
        qkv = x @ in_proj_w.T + in_proj_b
        q, k, v = jnp.split(qkv, 3, axis=-1)

        def heads(t):
            return t.reshape(B, N, H, D).transpose(0, 2, 1, 3)
        q, k, v = (heads(q), heads(k), heads(v))
        scores = jnp.einsum('bhnd,bhmd->bhnm', q, k) / jnp.sqrt(jnp.float32(D))
        scores = scores + mask[None, None]
        attn = jax.nn.softmax(scores, axis=-1)
        out = jnp.einsum('bhnm,bhmd->bhnd', attn, v)
        out = out.transpose(0, 2, 1, 3).reshape(B, N, E)
        return out @ out_w.T + out_b

    x = _layernorm(x + _L0_gnn_ref(x, adj, L0_gnn_a_0, L0_gnn_a_1, L0_gnn_a_2, L0_gnn_a_3), axis=-1)
    x = _layernorm(x + _L1_gnn_ref(x, adj, L1_gnn_in_proj_w, L1_gnn_in_proj_b, L1_gnn_out_w, L1_gnn_out_b), axis=-1)
    return x


_drawn_inputs = setup_inputs


def setup_inputs(seed=0):
    import zlib

    import numpy as np

    out = dict(_drawn_inputs(seed))
    spreads = {'L1_gnn_in_proj_b': (0.0, 0.1), 'L1_gnn_out_b': (0.0, 0.1)}
    factors = {}
    for name, (base, spread) in spreads.items():
        noise = np.random.default_rng([zlib.crc32(name.encode()), seed]).standard_normal(out[name].shape)
        drawn = base * np.exp(spread * noise) if base else spread * noise
        out[name] = jnp.asarray(drawn.astype(out[name].dtype))
    for name, factor in factors.items():
        out[name] = (out[name] * factor).astype(out[name].dtype)
    return out
```

```python
import concourse.bass as bass
from concourse import mybir
from contextlib import ExitStack

F32 = mybir.dt.float32
F32R = mybir.dt.float32r
BF16 = mybir.dt.bfloat16
I32 = mybir.dt.int32
ACT = mybir.ActivationFunctionType
ALU = mybir.AluOpType

B, N, D = 8, 2048, 128
HEADS, HD = 4, 32
P = 128
NT = N // P
TILES = B * NT
BANK = 512
HALF = N // 2
GROUPS = N // BANK
BLOCKS = BANK // P
KINDS = 4
LEAKY = 0.2
EPS = 1e-5
MASKED0 = -9.0e15 / LEAKY
MASKED1 = -1.0e9
STACK = 3 * HD
Q_SCALE = float(HD) ** -0.5


def wait_apart(engine, c, sem, value):
    if not isinstance(value, int):
        spare = c["spare", engine.engine]
        engine.reg_mov(spare, engine.to_reg(value))
        value = spare
    engine.wait_ge(c["made"], 2)
    engine.wait_ge(sem, value)


def scratch(nc):
    def dram(name, shape, dt):
        return nc.dram_tensor(f"kept_{name}", shape, dt, kind="Internal").ap()
    return dict(
        xt=dram("xt", [B + 2, D, 2 + 2 * KINDS, N], F32),
        x1v=dram("x1v", [TILES, P, 2, D], F32),
        stacks=dram("stacks", [TILES, 3, 2, D, P], F32),
        mask1=dram("mask1", [NT, P, N], BF16),
    )


def constants(nc, hold, io):
    def sb(name, shape, dt=F32):
        return hold.enter_context(nc.sbuf_tensor(f"c_{name}", shape, dt))
    c = dict(
        ident=sb("ident", [P, P]), a=sb("a", [D, KINDS]), w_qkv=sb("w_qkv", [D, 3 * D]), w_out=sb("w_out", [D, D]),
        b_qk=sb("b_qk", [D, 2]), b_q=sb("b_q", [D, 1]), b_v=sb("b_v", [P, D]), b_out=sb("b_out", [P, D]),
        half=sb("half", [P, 1]), minus1=sb("minus1", [P, 1]), high=sb("high", [P, 1]), ones=sb("ones", [P, 1]),
        general=sb("general", [1, 1], I32),
    )
    loaded = hold.enter_context(nc.semaphore("loaded"))
    made = c["made"] = hold.enter_context(nc.semaphore("made"))
    scaled = hold.enter_context(nc.semaphore("scaled"))
    for engine in (nc.vector, nc.gpsimd):
        c["spare", engine.engine] = engine.alloc_register("spare")
    with nc.Block() as block:
        @block.vector
        def _(dve):
            dve.reg_mov(c["spare", dve.engine], 0)

        @block.sync
        def _(sp):
            for dst, src in (("a", "a"), ("w_qkv", "w_qkv"), ("w_out", "w_out"), ("b_qk", "b_qk"),
                             ("b_v", "b_v"), ("b_out", "b_out")):
                sp.dma_start(c[dst][:], io[src]).then_inc(loaded, 16)
            sp.wait_ge(loaded, 6 * 16)
            sp.wait_ge(scaled, 1)

        @block.gpsimd
        def _(pool):
            pool.memset(c["ident"][:], 0.0).then_inc(made, 1)
            pool.memset(c["half"][:], -0.5)
            pool.memset(c["minus1"][:], -1.0)
            pool.memset(c["high"][:], 0.0)
            pool.memset(c["ones"][:], 1.0)
            pool.wait_ge(made, 1)
            pool.affine_select(out=c["ident"][:], in_=c["ident"][:], compare_op=ALU.not_equal, fill=1.0,
                               base=0, pattern=[[-1, P]], channel_multiplier=1).then_inc(made, 1)
            pool.wait_ge(made, 2)

        @block.scalar
        def _(act):
            act.wait_ge(loaded, 6 * 16)
            nc.scalar.mul(c["b_q"][:], c["b_qk"][:, 0:1], Q_SCALE).then_inc(scaled, 1)
    return c


def layer0(nc, io, dram, c, kinds, tag):
    with ExitStack() as hold:
        def sb(name, shape, dt=F32):
            return hold.enter_context(nc.sbuf_tensor(f"{tag}_{name}_", shape, dt))

        def ps(name, cols):
            return hold.enter_context(nc.psum_tensor(f"{tag}_{name}_", [P, cols], F32))

        def sem(name):
            return hold.enter_context(nc.semaphore(f"{tag}_{name}_"))

        def pair(f, name, *rest):
            return [f(f"{name}_{p}", *rest) for p in range(2)]

        first = kinds == 1
        PARTS = 2 + 2 * kinds
        x_in = pair(sb, "x_in", [P, D])
        xf = pair(sb, "xf", [D, P])
        ident16 = sb("ident16", [P, P], BF16)
        prep_f = sb("prep_f", [D, kinds, P])
        prep = pair(sb, "prep", [D, PARTS, P], F32R)
        q = pair(sb, "q", [D, 2 * kinds, P], F32R)
        xt = sb("xt", [D, 2, N], F32R)
        xv = sb("xv", [P, NT, D])
        adj = pair(sb, "adj", [P, N], I32)
        mask = pair(sb, "mask", [P, N], BF16)
        t = pair(sb, "t", [P, N])
        more = sb("more", [P, N]) if kinds > 1 else None
        part_max = pair(sb, "part_max", [P, 2 * kinds])
        row_max = pair(sb, "row_max", [P, 1])
        neg_max = pair(sb, "neg_max", [P, 1])
        row_sum = pair(sb, "row_sum", [P, 1])
        pt = sb("pt", [P, NT, P])
        x_res = pair(sb, "x_res", [P, D])
        inv_sum = sb("inv_sum", [P, 1])
        y = sb("y", [P, D])
        stats = sb("stats", [P, nc.vector.BN_STATS_DIM])
        mean_var = sb("mean_var", [P, 2])
        var_eps = sb("var_eps", [P, 1])
        rstd = sb("rstd", [P, 1])
        x1v = pair(sb, "x1v", [P, 2, D])
        x1t = sb("x1t", [D, P])
        qk_f = sb("qk_f", [D, 2, P])
        qk = pair(sb, "qk", [D, 4, P], F32R)
        junk = sb("junk", [P, N], BF16)
        above = pair(sb, "above", [P, 1])
        mask1 = sb("mask1", [P, N], BF16) if first else None

        scores = ps("scores", N)
        blocks = ps("blocks", 2 * BANK)
        av = ps("av", BANK)
        misc = ps("misc", BANK)

        x_loaded, q_loaded = pair(sem, "x_loaded"), pair(sem, "q_loaded")
        adj_loaded, res_loaded = pair(sem, "adj_loaded"), pair(sem, "res_loaded")
        xt_loaded = pair(sem, "xt_loaded")
        xv_loaded = [sem(f"xv_loaded{g}") for g in range(GROUPS)]
        prep_stored, tail_stored = pair(sem, "prep_stored"), pair(sem, "tail_stored")
        x_turned, x_copied, prep_f_done, prep_hi, prep_done = (sem(s) for s in (
            "x_turned", "x_copied", "prep_f_done", "prep_hi", "prep_done"))
        scored, slope_done, mask_done, part_done, merged, row_max_done, neg_max_done, prob_done = (sem(s) for s in (
            "scored", "slope_done", "mask_done", "part_done", "merged", "row_max_done", "neg_max_done", "prob_done"))
        turned, pt_act, pt_dve, av_done = (sem(s) for s in ("turned", "pt_act", "pt_dve", "av_done"))
        inv_done, y_done, stats_done, mv_done, eps_done, rstd_done, x1_done = (sem(s) for s in (
            "inv_done", "y_done", "stats_done", "mv_done", "eps_done", "rstd_done", "x1_done"))
        x1_turned, x1t_done, projected, qk_f_done, v_done, qk_hi, qk_done = (sem(s) for s in (
            "x1_turned", "x1t_done", "projected", "qk_f_done", "v_done", "qk_hi", "qk_done"))
        noted, high_done, ident16_done = sem("noted"), sem("high_done"), sem("ident16_done")
        mask1_done, mask1_stored = sem("mask1_done"), sem("mask1_stored")
        note_summed, note_done = sem("note_summed"), sem("note_done")

        ACT_GROUPS, DVE_GROUPS = (0, 1, 3), (2,)
        LEAD = NT + 2
        TAIL_STORES = 4
        LAG = 3

        x_tiles = io["x"].rearrange("b (t p) d -> (b t) p d", p=P)
        adj_tiles = io["adj"].rearrange("b (t p) m -> (b t) p m", p=P)

        def mask_of(k, p):
            return p if kinds == 1 else k % 2

        def row(ap, i):
            return ap[i] if isinstance(i, int) else ap[bass.ds(i, 1)].rearrange("a p d -> (a p) d")

        def xt_part(j, lo, hi):
            if isinstance(j, int):
                return dram["xt"][j // NT, :, lo:hi, j % NT * P:j % NT * P + P]
            return dram["xt"][bass.ds(j // NT, 1), :, lo:hi, bass.ds((j % NT) * P, P)].rearrange("a d k n -> (a d) k n")

        with nc.Block() as block:
            @block.sync
            def _(sp):
                def store_prep(j, p):
                    sp.wait_ge(prep_done, j + 1)
                    sp.dma_start(xt_part(j, 0, PARTS), prep[p][:].bitcast(F32)).then_inc(prep_stored[p], 16)

                def load_adj(i, p):
                    if not (isinstance(i, int) and i < 2):
                        sp.wait_ge(mask_done, (i - 1) * kinds)
                        if first:
                            sp.wait_ge(noted, i - 1)
                    sp.dma_start(adj[p][:], row(adj_tiles, i)).then_inc(adj_loaded[p], 16)

                def load_q(i, p, n):
                    if not (isinstance(i, int) and i < 2):
                        sp.wait_ge(scored, (i - 1) * (2 * kinds))
                    sp.wait_ge(prep_stored[p], n * 16)
                    sp.dma_start(q[p][:].bitcast(F32), xt_part(i, 2, PARTS)).then_inc(q_loaded[p], 16)

                def load_xt(b):
                    for p in range(2):
                        sp.wait_ge(prep_stored[p], (b + 1) * (NT // 2 * 16))
                    for h in range(2):
                        cols = slice(h * HALF, (h + 1) * HALF)
                        if isinstance(b, int):
                            src = dram["xt"][b, :, 0:2, cols]
                        else:
                            src = dram["xt"][bass.ds(b, 1), :, 0:2, cols].rearrange("a d k n -> (a d) k n")
                        if not (isinstance(b, int) and b == 0):
                            sp.wait_ge(scored, b * (NT * 2 * kinds) + (h - 1))
                        sp.dma_start(xt[:, :, cols].bitcast(F32), src).then_inc(xt_loaded[h], 16)

                def load_xv(b):
                    for g in range(GROUPS):
                        if isinstance(b, int):
                            src = x_tiles[b * NT + g * BLOCKS:b * NT + (g + 1) * BLOCKS]
                        else:
                            src = x_tiles[bass.ds(b * NT + g * BLOCKS, BLOCKS)]
                        if not (isinstance(b, int) and b == 0):
                            sp.wait_ge(av_done, b * (NT * GROUPS) + (g + 1 - GROUPS))
                        sp.dma_start(xv[:, g * BLOCKS:(g + 1) * BLOCKS, :],
                                     src.rearrange("t p d -> p t d")).then_inc(xv_loaded[g], 16)

                def store_mask1(i):
                    sp.wait_ge(mask1_done, i + 1)
                    sp.dma_start(dram["mask1"][i], mask1[:]).then_inc(mask1_stored, 16)

                def store_tail(i, p):
                    sp.wait_ge(x1_done, i + 1)
                    sp.wait_ge(v_done, i + 1)
                    static = isinstance(i, int)
                    sp.dma_start(dram["x1v"][i] if static else
                                 dram["x1v"][bass.ds(i, 1)].rearrange("a p w d -> (a p) w d"),
                                 x1v[p][:]).then_inc(tail_stored[p], 16)
                    sp.wait_ge(qk_done, i + 1)
                    to = dram["stacks"][i] if static else \
                        dram["stacks"][bass.ds(i, 1)].rearrange("a s w d n -> (a s) w d n")
                    for third, (q_part, k_part) in enumerate(((1, 2), (1, 3), (0, 2))):
                        sp.dma_start(to[third].rearrange("w d n -> d w n"),
                                     qk[p][:, q_part:k_part + 1:k_part - q_part, :].bitcast(F32)).then_inc(tail_stored[p], 16)

                def step(b, g, p, after_b=None):
                    i = b * NT + g * 2 + p
                    at = i if isinstance(i, int) else None
                    if at is None or at >= LAG:
                        store_tail(i - LAG, (p - LAG) % 2)
                    if at is None or at < TILES - 2:
                        load_q(i + 2, p, b * (NT // 2) + (g + 2))
                    if after_b is not None:
                        load_xt(after_b)
                    if at is None or at >= 2:
                        sp.wait_ge(y_done, i - 1)
                    sp.dma_start(x_res[p][:], row(x_tiles, i)).then_inc(res_loaded[p], 16)
                    sp.wait_ge(x_turned, i + (LEAD - 1))
                    sp.dma_start(x_in[p][:], row(x_tiles, (i + LEAD) % TILES)).then_inc(x_loaded[p], 16)
                    if at is None or at < TILES - 3:
                        load_adj(i + 3, 1 - p)
                    if at != 0:
                        store_prep(i + (LEAD - 1), 1 - p)
                    if first and at is not None and at < NT - 1:
                        store_mask1(at + 1)

                def graph(b, last=False):
                    step(b, 0, 0)
                    if not (isinstance(b, int) and b == 0):
                        load_xv(b)
                    step(b, 0, 1)
                    if isinstance(b, int) and b == 0:
                        for g in range(1, NT // 2 - 1):
                            for p in range(2):
                                step(b, g, p)
                    else:
                        with sp.Fori(1, NT // 2 - 2) as g:
                            for p in range(2):
                                step(b, g, p)
                        for p in range(2):
                            step(b, NT // 2 - 2, p)
                    step(b, NT // 2 - 1, 0)
                    step(b, NT // 2 - 1, 1, None if last else b + 1)

                load_adj(0, 0)
                load_adj(1, 1)
                for j in range(LEAD + 1):
                    if j < LEAD:
                        if j >= 2:
                            sp.wait_ge(x_turned, j - 1)
                        sp.dma_start(x_in[j % 2][:], x_tiles[j]).then_inc(x_loaded[j % 2], 16)
                    if j >= 1:
                        store_prep(j - 1, (j - 1) % 2)
                if first:
                    store_mask1(0)
                load_xt(0)
                load_q(0, 0, 1)
                load_q(1, 1, 1)
                load_xv(0)
                load_adj(2, 0)

                graph(0)
                with sp.Fori(1, B - 1) as b:
                    graph(b)
                graph(B - 1, last=True)
                for i in range(TILES - LAG, TILES):
                    store_tail(i, i % 2)
                for p in range(2):
                    sp.wait_ge(tail_stored[p], TILES // 2 * TAIL_STORES * 16)
                    sp.wait_ge(x_loaded[p], (TILES + LEAD) // 2 * 16)
                    sp.wait_ge(prep_stored[p], ((TILES + LEAD) // 2 - p) * 16)
                if first:
                    sp.wait_ge(mask1_stored, NT * 16)

            @block.gpsimd
            def _(pool):
                def split(j, p, stored):
                    if not (isinstance(j, int) and j < 2):
                        pool.wait_ge(prep_stored[p], stored)
                    if not (isinstance(j, int) and j == 0):
                        pool.wait_ge(prep_done, j)
                    wait_apart(pool, c, x_copied, j + 1)
                    nc.gpsimd.tensor_copy(prep[p][:, 0, :], xf[p][:])
                    for k in range(kinds):
                        last = nc.gpsimd.tensor_scalar(prep_f[:, k, :], xf[p][:], c["a"][:, k:k + 1], None, ALU.mult)
                    last.then_inc(prep_f_done, 1)
                    pool.wait_ge(prep_f_done, j + 1)
                    nc.gpsimd.tensor_tensor(prep[p][:, 1, :], xf[p][:], prep[p][:, 0, :].bitcast(F32), ALU.subtract)
                    nc.gpsimd.tensor_copy(prep[p][:, 2:2 + kinds, :], prep_f[:]).then_inc(prep_hi, 1)
                    pool.wait_ge(prep_hi, j + 1)
                    nc.gpsimd.tensor_tensor(prep[p][:, 2 + kinds:, :], prep_f[:], prep[p][:, 2:2 + kinds, :].bitcast(F32),
                                            ALU.subtract).then_inc(prep_done, 1)

                def root(i):
                    pool.wait_ge(eps_done, i + 1)
                    nc.gpsimd.tensor_tensor(rstd[:], var_eps[:], c["half"][:], ALU.pow).then_inc(rstd_done, 1)

                def split_qk(i, p, start):
                    if not start:
                        pool.wait_ge(tail_stored[p], tail_count(i, p))
                    wait_apart(pool, c, qk_f_done, 2 * i + 2)
                    nc.gpsimd.tensor_copy(qk[p][:, 1:3, :], qk_f[:]).then_inc(qk_hi, 1)
                    pool.wait_ge(qk_hi, i + 1)
                    nc.gpsimd.tensor_tensor(qk[p][:, 0:4:3, :], qk_f[:], qk[p][:, 1:3, :].bitcast(F32),
                                            ALU.subtract).then_inc(qk_done, 1)

                def tail_count(i, p):
                    return (i - p) * (TAIL_STORES // 2 * 16)                 

                nc.gpsimd.tensor_copy(ident16[:], c["ident"][:]).then_inc(ident16_done, 1)
                for j in range(LEAD):
                    split(j, j % 2, (j // 2) * 16)

                def step(i, p, start):
                    if not start:
                        root(i - 1)
                    split(i + LEAD, p, (i - p) * 8 + LEAD // 2 * 16)
                    if first:
                        pool.wait_ge(noted, i + 1)
                        nc.gpsimd.tensor_tensor(c["high"][:], c["high"][:], above[p][:], ALU.add).then_inc(high_done, 1)
                    if not start:
                        split_qk(i - 1, 1 - p, isinstance(i, int) and i < 3)

                step(0, 0, True)
                step(1, 1, False)
                step(2, 0, False)
                step(3, 1, False)
                with pool.Fori(2, TILES // 2) as g:
                    for p in range(2):
                        step(g * 2 + p, p, False)
                root(TILES - 1)
                split_qk(TILES - 1, 1, False)

            @block.tensor
            def _(pe):
                def turn_x(j, p, n):
                    pe.wait_ge(x_loaded[p], 16 * n)
                    nc.tensor.transpose(misc[:, 0:P], x_in[p][:], c["ident"][:]).then_inc(x_turned, 1)

                def score(i, p, b, n, parts, start=False):
                    if 0 in parts:
                        pe.wait_ge(q_loaded[p], 16 * n)
                    for part in parts:
                        for k, h in [divmod(part, 2)]:
                            if k == 0:
                                pe.wait_ge(xt_loaded[h], (b + 1) * 16)
                            if not (start and k == 0):
                                pe.wait_ge(part_done, i * (2 * kinds) + (2 * k + h - 1))
                            for s, (q_part, x_part) in enumerate(((k, 0), (k, 1), (kinds + k, 0))):
                                for bank in range(2):
                                    at = h * HALF + bank * BANK
                                    nc.tensor.matmul(scores[:, at:at + BANK], q[p][:, q_part, :],
                                                     xt[:, x_part, at:at + BANK], start=(s == 0), stop=False)
                            if h == 0:
                                pe.wait_ge(mask_done, i * kinds + (k + 1))
                            for bank in range(2):
                                at = h * HALF + bank * BANK
                                last = nc.tensor.matmul(scores[:, at:at + BANK], ident16[:], mask[mask_of(k, p)][:, at:at + BANK],
                                                        start=False, stop=True)
                            last.then_inc(scored, 1)

                def turn(i, p, g, start):
                    if g == 0:
                        pe.wait_ge(prob_done, i + 1)
                    if not (start and g < 2):
                        free_of(i, g)
                    for k in range(BLOCKS):
                        m = g * BLOCKS + k
                        last = nc.tensor.transpose(blocks[:, (g % 2) * BANK + k * P:(g % 2) * BANK + (k + 1) * P],
                                                   t[p][:, m * P:(m + 1) * P], c["ident"][:])
                    last.then_inc(turned, 1)

                def free_of(i, g):
                    prev, tile = (g - 2, i) if g >= 2 else (g + 2, i - 1)
                    wait_pt(tile, prev)

                def wait_pt(tile, g):
                    if g in ACT_GROUPS:
                        pe.wait_ge(pt_act, tile * len(ACT_GROUPS) + (ACT_GROUPS.index(g) + 1))
                    else:
                        pe.wait_ge(pt_dve, tile * len(DVE_GROUPS) + (DVE_GROUPS.index(g) + 1))

                def values(i, g, b, start):
                    if g == 0:
                        if not start:
                            pe.wait_ge(y_done, i)
                    pe.wait_ge(xv_loaded[g], (b + 1) * 16)
                    wait_pt(i, g)
                    for k in range(BLOCKS):
                        m = g * BLOCKS + k
                        last = nc.tensor.matmul(av[:, 0:D], pt[:, m, :], xv[:, m, :], start=(m == 0), stop=(m == NT - 1))
                    last.then_inc(av_done, 1)

                def turn_x1(i, p):
                    pe.wait_ge(x1_done, i + 1)
                    pe.wait_ge(x_copied, misc_preps(i))
                    nc.tensor.transpose(misc[:, P:2 * P], x1v[p][:, 0, :], c["ident"][:]).then_inc(x1_turned, 1)

                def misc_preps(i):
                    return i + (LEAD + 2) if not (isinstance(i, int) and i == TILES - 1) else TILES + LEAD

                def project(i):
                    pe.wait_ge(x1t_done, i + 1)
                    for w in range(2):
                        nc.tensor.matmul(misc[:, w * P:(w + 1) * P], c["w_qkv"][:, w * D:(w + 1) * D], x1t[:],
                                         start=True, stop=True)
                    nc.tensor.matmul(misc[:, 2 * P:3 * P], x1t[:], c["w_qkv"][:, 2 * D:3 * D],
                                     start=True, stop=True).then_inc(projected, 1)

                for j in range(LEAD):
                    if j:
                        pe.wait_ge(x_copied, j)
                    turn_x(j, j % 2, j // 2 + 1)
                pe.wait_ge(ident16_done, 1)
                score(0, 0, 0, 1, range(2 * kinds), start=True)

                def step(i, p, g, start, end=False):
                    b = g // (NT // 2)
                    nb = b if p == 0 else (g + 1) // (NT // 2)
                    early, late = (range(1), range(1, 2)) if kinds == 1 else ((), range(2 * kinds))
                    if not end:
                        score(i + 1, 1 - p, nb, g + 1 + p, early)
                    if start:
                        pe.wait_ge(x_copied, LEAD)
                    elif not (isinstance(i, int) and i < 2):
                        pe.wait_ge(qk_f_done, 2 * (i - 1))
                        pe.wait_ge(v_done, i - 1)
                    turn_x(i + LEAD, p, LEAD // 2 + 1 + g)
                    turn(i, p, 0, start)
                    turn(i, p, 1, start)
                    if not end:
                        score(i + 1, 1 - p, nb, g + 1 + p, late)
                    if not start:
                        turn_x1(i - 1, 1 - p)
                    values(i, 0, b, start)
                    turn(i, p, 2, start)
                    values(i, 1, b, start)
                    turn(i, p, 3, start)
                    if not start:
                        project(i - 1)
                    values(i, 2, b, start)
                    values(i, 3, b, start)

                step(0, 0, 0, True)
                step(1, 1, 0, False)
                with pe.Fori(1, TILES // 2 - 1) as g:
                    for p in range(2):
                        step(g * 2 + p, p, g, False)
                g = TILES // 2 - 1
                step(2 * g, 0, g, False)
                step(2 * g + 1, 1, g, False, end=True)
                pe.wait_ge(qk_f_done, 2 * (TILES - 1))
                pe.wait_ge(v_done, TILES - 1)
                turn_x1(TILES - 1, 1)
                project(TILES - 1)
                if first:
                    pe.wait_ge(high_done, TILES)
                    nc.tensor.matmul(av[0:1, 0:1], c["high"][:], c["ones"][:], start=True, stop=True).then_inc(note_summed, 1)

            @block.scalar
            def _(act):
                def slope(i, p, start, parts=range(2 * kinds)):
                    if not start and 0 in parts:
                        act.wait_ge(turned, (i - 1) * GROUPS)
                    for part in parts:
                        k, h = divmod(part, 2)
                        act.wait_ge(scored, i * (2 * kinds) + (part + 1))
                        dst = more if k else t[p]
                        if k and not (isinstance(i, int) and i == 0 and k == 1):
                            act.wait_ge(merged, i * (2 * (kinds - 1)) + (2 * (k - 1) + h - 1))
                        nc.scalar.activation(dst[:, h * HALF:(h + 1) * HALF], scores[:, h * HALF:(h + 1) * HALF],
                                             ACT.Relu, scale=1.0 / LEAKY - 1.0).then_inc(slope_done, 1)

                def copy_blocks(i, g):
                    act.wait_ge(turned, i * GROUPS + (g + 1))
                    nc.scalar.activation(pt[:, g * BLOCKS:(g + 1) * BLOCKS, :].rearrange("p m n -> p (m n)"),
                                         blocks[:, (g % 2) * BANK:(g % 2 + 1) * BANK], ACT.Copy).then_inc(pt_act, 1)

                def probabilities(i, p, start):
                    act.wait_ge(neg_max_done, i + 1)
                    if not start:
                        act.wait_ge(inv_done, i - 1)
                    nc.scalar.activation(t[p][:], t[p][:], ACT.Exp, bias=neg_max[p][:],
                                         accum_out=row_sum[p][:]).then_inc(prob_done, 1)

                def note(i, p, n, start):
                    act.wait_ge(adj_loaded[p], 16 * n)
                    if not start:
                        act.wait_ge(high_done, i - 1)
                    if not (isinstance(i, int) and i == 0):
                        act.wait_ge(noted, i)
                    nc.scalar.activation(junk[:], adj[p][:], ACT.Relu, bias=c["minus1"][:],
                                         accum_out=above[p][:]).then_inc(noted, 1)

                def qk_bias(i, start):
                    act.wait_ge(projected, i + 1)
                    if not start:
                        act.wait_ge(qk_done, i)
                    nc.scalar.activation(qk_f[:, 0, :], misc[:, 0:P], ACT.Identity, bias=c["b_q"][:],
                                         scale=Q_SCALE).then_inc(qk_f_done, 1)
                    nc.scalar.activation(qk_f[:, 1, :], misc[:, P:2 * P], ACT.Identity,
                                         bias=c["b_qk"][:, 1:2]).then_inc(qk_f_done, 1)

                slope(0, 0, True)
                probabilities(0, 0, True)
                if first:
                    note(0, 0, 1, True)
                    note(1, 1, 1, True)

                def step(i, p, g, start, end=False):
                    early, late = (range(1), range(1, 2)) if kinds == 1 else ((), range(2 * kinds))
                    if not end:
                        slope(i + 1, 1 - p, start, early)
                    for k in ACT_GROUPS[:-1]:
                        copy_blocks(i, k)
                    if not end:
                        slope(i + 1, 1 - p, start, late)
                    copy_blocks(i, ACT_GROUPS[-1])
                    if not end:
                        probabilities(i + 1, 1 - p, start)
                    if not start:
                        qk_bias(i - 1, isinstance(i, int) and i == 1)
                    if first and not (isinstance(i, int) and i >= TILES - 2):
                        note(i + 2, p, g + 2, False)

                step(0, 0, 0, True)
                step(1, 1, 0, False)
                with act.Fori(1, TILES // 2 - 1) as g:
                    for p in range(2):
                        step(g * 2 + p, p, g, False)
                g = TILES // 2 - 1
                step(2 * g, 0, g, False)
                step(2 * g + 1, 1, g, False, end=True)
                qk_bias(TILES - 1, False)

            @block.vector
            def _(dve):
                def copy_x(j, p, start):
                    dve.wait_ge(x_turned, j + 1)
                    if not start:
                        dve.wait_ge(prep_done, j - 1)
                    nc.vector.tensor_copy(xf[p][:], misc[:, 0:P]).then_inc(x_copied, 1)

                def make_mask(i, k, p, n, start, make1=False):
                    if k == 0:
                        dve.wait_ge(adj_loaded[p], 16 * n)
                    if make1:
                        if not (isinstance(i, int) and i == 0):
                            dve.wait_ge(mask1_stored, i * 16)
                        nc.vector.tensor_scalar(mask1[:], adj[p][:], 0.0, MASKED1, ALU.is_equal,
                                                ALU.mult).then_inc(mask1_done, 1)
                    if not start:
                        dve.wait_ge(scored, (i * kinds + k - 1) * 2)
                    nc.vector.tensor_scalar(mask[mask_of(k, p)][:], adj[p][:], float(k + 1), MASKED0, ALU.not_equal,
                                            ALU.mult).then_inc(mask_done, 1)

                def masked_max(i, p, n, start, parts=range(2 * kinds)):
                    for part in parts:
                        k, h = divmod(part, 2)
                        if kinds > 1 and part == 0:
                            make_mask(i, 0, p, n, start)
                        if h == 0 and 1 <= k + 1 < kinds:
                            make_mask(i, k + 1, p, n, start and k + 1 < 2)
                        dst = more if k else t[p]
                        wait_apart(dve, c, slope_done, i * (2 * kinds) + (part + 1))
                        cols = slice(h * HALF, (h + 1) * HALF)
                        nc.vector.tensor_tensor_reduce(
                            out=dst[:, cols], in0=scores[:, cols], in1=dst[:, cols], scale=LEAKY, scalar=-3.0e38,
                            op0=ALU.add, op1=ALU.max, accum_out=part_max[p][:, part:part + 1]).then_inc(part_done, 1)
                        if k:
                            dve.wait_ge(part_done, i * (2 * kinds) + (part + 1))
                            nc.vector.tensor_tensor(t[p][:, cols], t[p][:, cols], more[:, cols],
                                                    ALU.max).then_inc(merged, 1)
                    if 2 * kinds - 1 not in parts:
                        return
                    dve.wait_ge(part_done, i * (2 * kinds) + (2 * kinds))
                    if kinds > 1:
                        nc.vector.reduce_max(row_max[p][:], part_max[p][:], axis=mybir.AxisListType.X).then_inc(row_max_done, 1)
                        dve.wait_ge(row_max_done, i + 1)
                        nc.vector.tensor_scalar(neg_max[p][:], row_max[p][:], -1.0, None, ALU.mult).then_inc(neg_max_done, 1)
                    else:
                        nc.vector.tensor_scalar(neg_max[p][:], part_max[p][:, 0:1], part_max[p][:, 1:2], -1.0,
                                                ALU.max, ALU.mult).then_inc(neg_max_done, 1)

                def copy_blocks(i, g):
                    dve.wait_ge(turned, i * GROUPS + (g + 1))
                    nc.vector.tensor_copy(pt[:, g * BLOCKS:(g + 1) * BLOCKS, :].rearrange("p m n -> p (m n)"),
                                          blocks[:, (g % 2) * BANK:(g % 2 + 1) * BANK]).then_inc(pt_dve, 1)

                def norm(i, p, n, start):
                    dve.wait_ge(prob_done, i + 1)
                    nc.vector.reciprocal(inv_sum[:], row_sum[p][:]).then_inc(inv_done, 1)
                    dve.wait_ge(inv_done, i + 1)
                    dve.wait_ge(res_loaded[p], 16 * n)
                    dve.wait_ge(av_done, (i + 1) * GROUPS)
                    nc.vector.scalar_tensor_tensor(out=y[:], in0=av[:, 0:D], scalar=inv_sum[:], in1=x_res[p][:],
                                                   op0=ALU.mult, op1=ALU.add).then_inc(y_done, 1)
                    dve.wait_ge(y_done, i + 1)
                    nc.vector.bn_stats(out=stats[:], in_=y[:]).then_inc(stats_done, 1)
                    wait_apart(dve, c, stats_done, i + 1)
                    nc.vector.bn_aggr(out=mean_var[:], in_=stats[:]).then_inc(mv_done, 1)
                    dve.wait_ge(mv_done, i + 1)
                    nc.vector.tensor_scalar(var_eps[:], mean_var[:, 1:2], EPS, None, ALU.add).then_inc(eps_done, 1)

                def finish_norm(i, p, start):
                    dve.wait_ge(rstd_done, i + 1)
                    if not start:
                        dve.wait_ge(tail_stored[p], (i - p) * (TAIL_STORES // 2 * 16))
                    nc.vector.tensor_scalar(x1v[p][:, 0, :], y[:], mean_var[:, 0:1], rstd[:], ALU.subtract,
                                            ALU.mult).then_inc(x1_done, 1)

                def copy_x1t(i):
                    dve.wait_ge(x1_turned, i + 1)
                    nc.vector.tensor_copy(x1t[:], misc[:, P:2 * P]).then_inc(x1t_done, 1)

                def v_bias(i, p):
                    dve.wait_ge(projected, i + 1)
                    dve.wait_ge(qk_f_done, 2 * (i + 1))
                    nc.vector.tensor_tensor(x1v[p][:, 1, :], misc[:, 2 * P:3 * P], c["b_v"][:], ALU.add).then_inc(v_done, 1)

                for j in range(LEAD):
                    copy_x(j, j % 2, j < 2)
                if kinds == 1:
                    make_mask(0, 0, 0, 1, True, make1=True)
                    make_mask(1, 0, 1, 1, True, make1=True)
                masked_max(0, 0, 1, True)

                def step(i, p, g, start, end=False, make1=False):
                    if not start:
                        norm(i - 1, 1 - p, g + p, False)
                    copy_x(i + LEAD, p, False)
                    if not start:
                        finish_norm(i - 1, 1 - p, isinstance(i, int) and i < 3)
                    early, late = (range(1), range(1, 2)) if kinds == 1 else (range(2 * kinds), ())
                    if not end:
                        masked_max(i + 1, 1 - p, g + 1 + p, isinstance(i, int) and i == 0, early)
                    if not start:
                        copy_x1t(i - 1)
                    if not end:
                        masked_max(i + 1, 1 - p, g + 1 + p, isinstance(i, int) and i == 0, late)
                    for k in DVE_GROUPS:
                        copy_blocks(i, k)
                    if kinds == 1 and not (isinstance(i, int) and i >= TILES - 2):
                        make_mask(i + 2, 0, p, g + 2, False, make1)
                    if not start:
                        v_bias(i - 1, 1 - p)

                step(0, 0, 0, True, make1=first)
                step(1, 1, 0, False, make1=first)
                step(2, 0, 1, False, make1=first)
                step(3, 1, 1, False, make1=first)
                with dve.Fori(2, NT // 2 - 1) as g:
                    for p in range(2):
                        step(g * 2 + p, p, g, False, make1=first)
                g = NT // 2 - 1
                step(2 * g, 0, g, False)
                step(2 * g + 1, 1, g, False)
                with dve.Fori(NT // 2, TILES // 2 - 1) as g:
                    for p in range(2):
                        step(g * 2 + p, p, g, False)
                g = TILES // 2 - 1
                step(2 * g, 0, g, False)
                step(2 * g + 1, 1, g, False, end=True)
                norm(TILES - 1, 1, TILES // 2, False)
                finish_norm(TILES - 1, 1, False)
                copy_x1t(TILES - 1)
                v_bias(TILES - 1, 1)
                if first:
                    dve.wait_ge(note_summed, 1)
                    nc.vector.tensor_scalar(c["general"][:], av[0:1, 0:1], 0.0, None, ALU.is_gt).then_inc(note_done, 1)
                    dve.wait_ge(note_done, 1)


def layer1(nc, dram, c, out):
    with ExitStack() as hold:
        def sb(name, shape, dt=F32):
            return hold.enter_context(nc.sbuf_tensor(f"l1_{name}_", shape, dt))

        def ps(name, cols):
            return hold.enter_context(nc.psum_tensor(f"l1_{name}_", [P, cols], F32))

        def sem(name):
            return hold.enter_context(nc.semaphore(f"l1_{name}_"))

        def pair(f, name, *rest):
            return [f(f"{name}_{p}", *rest) for p in range(2)]

        q = sb("q", [STACK, HEADS, P], F32R)
        keys = sb("keys", [STACK, HEADS, N], F32R)
        v = sb("v", [P, NT, D])
        mask = pair(sb, "mask", [P, N], BF16)
        t = sb("t", [P, HEADS, N])
        part_max = sb("part_max", [P, HEADS, 2])
        neg_max = sb("neg_max", [P, HEADS])
        row_sum = pair(sb, "row_sum", [P, HEADS])
        pt = pair(sb, "pt", [P, HEADS, NT, P])
        inv_sum = sb("inv_sum", [P, HEADS])
        inv_wide = sb("inv_wide", [P, HEADS, HD])
        inv_t = sb("inv_t", [D, P])
        o_t = sb("o_t", [D, P])
        x1 = pair(sb, "x1", [P, D])
        res = pair(sb, "res", [P, D])
        z = sb("z", [P, D])
        stats = sb("stats", [P, nc.vector.BN_STATS_DIM])
        mean_var = sb("mean_var", [P, 2])
        var_eps = sb("var_eps", [P, 1])
        rstd = sb("rstd", [P, 1])
        normed = pair(sb, "normed", [P, D])

        scores = ps("scores", N)
        blocks = ps("blocks", 2 * BANK)
        av = ps("av", BANK)
        misc = ps("misc", BANK)

        q_loaded = [sem(f"q_loaded{h}") for h in range(HEADS)]
        keys_loaded = [sem(f"keys_loaded{h}") for h in range(HEADS)]
        v_loaded = [sem(f"v_loaded{g}") for g in range(GROUPS)]
        mask_loaded, x1_loaded, out_stored = pair(sem, "mask_loaded"), pair(sem, "x1_loaded"), pair(sem, "out_stored")
        scored, part_done, neg_max_done, prob_done = (sem(s) for s in ("scored", "part_done", "neg_max_done", "prob_done"))
        turned, pt_act, pt_dve, av_done = (sem(s) for s in ("turned", "pt_act", "pt_dve", "av_done"))
        inv_done, wide_done, wide_turned, inv_t_done, o_done = (sem(s) for s in (
            "inv_done", "wide_done", "wide_turned", "inv_t_done", "o_done"))
        projected, res_done, z_done, stats_done, mv_done, eps_done, rstd_done, normed_done = (sem(s) for s in (
            "projected", "res_done", "z_done", "stats_done", "mv_done", "eps_done", "rstd_done", "normed_done"))

        COPIES = ("ADAA",) * HEADS
        LAG = 3

        def copied(i, h, g):
            who = COPIES[h][g]
            before = sum(x.count(who) for x in COPIES[:h]) + COPIES[h][:g + 1].count(who)
            return (pt_act if who == "A" else pt_dve), i * sum(x.count(who) for x in COPIES) + before

        def static(i):
            return isinstance(i, int)

        out_tiles = out.rearrange("b (t p) d -> (b t) p d", p=P)

        def row(ap, i):
            return ap[i] if static(i) else ap[bass.ds(i, 1)].rearrange("a p d -> (a p) d")

        with nc.Block() as block:
            @block.sync
            def _(sp):
                def load_q(i, h):
                    if not (static(i) and i == 0):
                        sp.wait_ge(scored, i * (2 * HEADS) + (2 * h + 2 - 2 * HEADS))
                    for third in range(3):
                        src = dram["stacks"][i, third, 0, h * HD:(h + 1) * HD] if static(i) else \
                            dram["stacks"][bass.ds(i, 1), third, 0, h * HD:(h + 1) * HD].rearrange("a d n -> (a d) n")
                        sp.dma_start(q[third * HD:(third + 1) * HD, h, :].bitcast(F32), src).then_inc(q_loaded[h], 16)

                def load_keys(b, h):
                    for third in range(3):
                        src = dram["stacks"][b * NT:(b + 1) * NT, third, 1, h * HD:(h + 1) * HD] if static(b) else \
                            dram["stacks"][bass.ds(b * NT, NT), third, 1, h * HD:(h + 1) * HD]
                        sp.dma_start(keys[third * HD:(third + 1) * HD, h, :].rearrange("d (t n) -> d t n", n=P).bitcast(F32),
                                     src.rearrange("t d n -> d t n")).then_inc(keys_loaded[h], 16)

                def load_mask(i, p):
                    if not (static(i) and i < 2):
                        sp.wait_ge(part_done, (i - 1) * (2 * HEADS))
                    sp.dma_start(mask[p][:], row(dram["mask1"], i % NT)).then_inc(mask_loaded[p], 16)

                def load_v(b):
                    for g in range(GROUPS):
                        if static(b):
                            src = dram["x1v"][b * NT + g * BLOCKS:b * NT + (g + 1) * BLOCKS, :, 1, :]
                        else:
                            src = dram["x1v"][bass.ds(b * NT + g * BLOCKS, BLOCKS), :, 1, :]
                        if not (static(b) and b == 0):
                            sp.wait_ge(av_done, b * (NT * GROUPS) + (g + 1 - GROUPS))
                        sp.dma_start(v[:, g * BLOCKS:(g + 1) * BLOCKS, :],
                                     src.rearrange("t p d -> p t d")).then_inc(v_loaded[g], 16)

                def load_x1(i, p):
                    if not (static(i) and i < 2):
                        sp.wait_ge(res_done, i - 1)
                    src = dram["x1v"][i, :, 0, :] if static(i) else \
                        dram["x1v"][bass.ds(i, 1), :, 0, :].rearrange("a p d -> (a p) d")
                    sp.dma_start(x1[p][:], src).then_inc(x1_loaded[p], 16)

                def store(i, p):
                    sp.wait_ge(normed_done, i + 1)
                    sp.dma_start(row(out_tiles, i), normed[p][:]).then_inc(out_stored[p], 16)

                def step(b, nt, p, load_after=False, first_of=False):
                    i = b * NT + nt
                    if not (static(i) and i < LAG):
                        store(i - LAG, (p - LAG) % 2)
                    for h in range(HEADS):
                        if not (static(i) and i == TILES - 1):
                            load_q(i + 1, h)
                        if load_after:
                            load_keys(b + 1, h)
                    load_x1(i, p)
                    if not (static(i) and i >= TILES - 2):
                        load_mask(i + 2, p)
                    if first_of and not (static(b) and b == 0):
                        load_v(b)

                def graph(b, last=False):
                    step(b, 0, 0, first_of=True)
                    step(b, 1, 1)
                    if static(b) and b == 0:
                        for nt in range(2, NT - 2):
                            step(b, nt, nt % 2)
                    else:
                        with sp.Fori(1, NT // 2 - 1) as g:
                            for p in range(2):
                                step(b, g * 2 + p, p)
                    step(b, NT - 2, 0)
                    step(b, NT - 1, 1, load_after=not last)

                for h in range(HEADS):
                    load_q(0, h)
                    load_keys(0, h)
                    if h == 0:
                        load_mask(0, 0)
                load_mask(1, 1)
                load_v(0)
                graph(0)
                with sp.Fori(1, B - 1) as b:
                    graph(b)
                graph(B - 1, last=True)
                for i in range(TILES - LAG, TILES):
                    store(i, i % 2)
                for p in range(2):
                    sp.wait_ge(out_stored[p], TILES // 2 * 16)

            @block.gpsimd
            def _(pool):
                def residual(i, p, n):
                    pool.wait_ge(x1_loaded[p], 16 * n)
                    if not (static(i) and i < 2):
                        pool.wait_ge(z_done, i - 1)
                    nc.gpsimd.tensor_tensor(res[p][:], x1[p][:], c["b_out"][:], ALU.add).then_inc(res_done, 1)

                def root(i):
                    pool.wait_ge(eps_done, i + 1)
                    nc.gpsimd.tensor_tensor(rstd[:], var_eps[:], c["half"][:], ALU.pow).then_inc(rstd_done, 1)

                residual(0, 0, 1)
                residual(1, 1, 1)
                with pool.Fori(1, TILES // 2) as g:
                    for p in range(2):
                        residual(g * 2 + p, p, g + 1)
                        root(g * 2 + (p - 2))
                root(TILES - 2)
                root(TILES - 1)

            @block.tensor
            def _(pe):
                def score(i, h, half):
                    if half == 0:
                        pe.wait_ge(q_loaded[h], i * 48 + 48)
                        pe.wait_ge(keys_loaded[h], (i // NT) * 48 + 48)
                    if not (static(i) and i == 0 and h == 0):
                        pe.wait_ge(part_done, i * (2 * HEADS) + (2 * h + half - 1))
                    for bank in range(2):
                        at = half * HALF + bank * BANK
                        last = nc.tensor.matmul(scores[:, at:at + BANK], q[:, h, :], keys[:, h, at:at + BANK],
                                                start=True, stop=True)
                    last.then_inc(scored, 1)

                def turn(i, h, g):
                    if g == 0:
                        pe.wait_ge(prob_done, i * HEADS + (h + 1))
                    if g >= 2:
                        pe.wait_ge(*copied(i, h, g - 2))
                    elif h:
                        pe.wait_ge(*copied(i, h - 1, g + 2))
                    elif not (static(i) and i == 0):
                        pe.wait_ge(*copied(i - 1, HEADS - 1, g + 2))
                    for k in range(BLOCKS):
                        m = g * BLOCKS + k
                        last = nc.tensor.transpose(blocks[:, (g % 2) * BANK + k * P:(g % 2) * BANK + (k + 1) * P],
                                                   t[:, h, m * P:(m + 1) * P], c["ident"][:])
                    last.then_inc(turned, 1)

                def values(i, p, g):
                    if g == 0:
                        if not (static(i) and i == 0):
                            pe.wait_ge(o_done, i)
                        for who in "AD":
                            pe.wait_ge(*copied(i, HEADS - 1, COPIES[-1].rindex(who)))
                    pe.wait_ge(v_loaded[g], (i // NT) * 16 + 16)
                    for k in range(BLOCKS):
                        m = g * BLOCKS + k
                        for h in range(HEADS):
                            lanes = slice(h * HD, (h + 1) * HD)
                            last = nc.tensor.matmul(av[lanes, 0:P], v[:, m, lanes], pt[p][:, h, m, :],
                                                    start=(m == 0), stop=(m == NT - 1))
                    last.then_inc(av_done, 1)

                def turn_wide(i):
                    pe.wait_ge(wide_done, i + 1)
                    if not (static(i) and i < 2):
                        pe.wait_ge(z_done, i - 1)
                    nc.tensor.transpose(misc[:, 0:P], inv_wide[:].rearrange("p h d -> p (h d)"),
                                        c["ident"][:]).then_inc(wide_turned, 1)

                def project(i, last=False):
                    pe.wait_ge(o_done, i + 1)
                    pe.wait_ge(inv_t_done, TILES if last else i + 2)
                    nc.tensor.matmul(misc[:, P:2 * P], o_t[:], c["w_out"][:], start=True, stop=True).then_inc(projected, 1)

                def step(i, p):
                    for h in range(HEADS):
                        ahead = (i, h + 2) if h < 2 else (i + 1, h - 2)
                        more = not (static(i) and i == TILES - 1 and h >= 2)
                        turn(i, h, 0)
                        turn(i, h, 1)
                        if more:
                            score(*ahead, 0)
                        turn(i, h, 2)
                        turn(i, h, 3)
                        if more:
                            score(*ahead, 1)
                        if h == 0 and not (static(i) and i == 0):
                            turn_wide(i - 1)
                        if not (static(i) and i == 0):
                            values(i - 1, 1 - p, h)
                        if h == 1 and not (static(i) and i < 2):
                            project(i - 2)

                for h in range(2):
                    for half in range(2):
                        score(0, h, half)
                for i in range(4):
                    step(i, i % 2)
                with pe.Fori(2, TILES // 2 - 1) as g:
                    for p in range(2):
                        step(g * 2 + p, p)
                step(TILES - 2, 0)
                step(TILES - 1, 1)
                turn_wide(TILES - 1)
                for g in range(GROUPS):
                    values(TILES - 1, 1, g)
                project(TILES - 2)
                pe.wait_ge(z_done, TILES - 1)
                project(TILES - 1, last=True)

            @block.scalar
            def _(act):
                def probabilities(i, p, h):
                    act.wait_ge(neg_max_done, i * HEADS + (h + 1))
                    if h == 0 and not (static(i) and i < 2):
                        act.wait_ge(inv_done, i - 1)
                    nc.scalar.activation(t[:, h, :], t[:, h, :], ACT.Exp, bias=neg_max[:, h:h + 1],
                                         accum_out=row_sum[p][:, h:h + 1]).then_inc(prob_done, 1)

                def copy_blocks(i, p, h, g):
                    act.wait_ge(turned, i * (HEADS * GROUPS) + (h * GROUPS + g + 1))
                    nc.scalar.activation(pt[p][:, h, g * BLOCKS:(g + 1) * BLOCKS, :].rearrange("p m n -> p (m n)"),
                                         blocks[:, (g % 2) * BANK:(g % 2 + 1) * BANK], ACT.Copy).then_inc(pt_act, 1)

                def copy_inv(i):
                    act.wait_ge(wide_turned, i + 1)
                    if not (static(i) and i == 0):
                        act.wait_ge(o_done, i)
                    nc.scalar.activation(inv_t[:], misc[:, 0:P], ACT.Copy).then_inc(inv_t_done, 1)

                def step(i, p):
                    for h in range(HEADS):
                        mine = [g for g in range(GROUPS) if COPIES[h][g] == "A"]
                        if h == 1 and not (static(i) and i == 0):
                            copy_inv(i - 1)
                        copy_blocks(i, p, h, mine[0])
                        if not (static(i) and i == TILES - 1 and h == HEADS - 1):
                            if h < HEADS - 1:
                                probabilities(i, p, h + 1)
                            else:
                                probabilities(i + 1, 1 - p, 0)
                        for g in mine[1:]:
                            copy_blocks(i, p, h, g)

                probabilities(0, 0, 0)
                step(0, 0)
                step(1, 1)
                with act.Fori(1, TILES // 2 - 1) as g:
                    for p in range(2):
                        step(g * 2 + p, p)
                step(TILES - 2, 0)
                step(TILES - 1, 1)
                copy_inv(TILES - 1)

            @block.vector
            def _(dve):
                def masked(i, p, h, half, n):
                    if h == 0 and half == 0:
                        dve.wait_ge(mask_loaded[p], 16 * n)
                    if half == 0 and not (static(i) and i == 0):
                        dve.wait_ge(turned, i * (HEADS * GROUPS) + ((h + 1) * GROUPS - HEADS * GROUPS))
                    wait_apart(dve, c, scored, i * (2 * HEADS) + (2 * h + half + 1))
                    cols = slice(half * HALF, (half + 1) * HALF)
                    nc.vector.tensor_tensor_reduce(
                        out=t[:, h, cols], in0=scores[:, cols], in1=mask[p][:, cols], scale=1.0, scalar=-3.0e38,
                        op0=ALU.add, op1=ALU.max, accum_out=part_max[:, h, half:half + 1]).then_inc(part_done, 1)

                def negate(i, h):
                    dve.wait_ge(part_done, i * (2 * HEADS) + (2 * h + 2))
                    nc.vector.tensor_scalar(neg_max[:, h:h + 1], part_max[:, h, 0:1], part_max[:, h, 1:2], -1.0,
                                            ALU.max, ALU.mult).then_inc(neg_max_done, 1)

                def copy_blocks(i, p, h, g):
                    dve.wait_ge(turned, i * (HEADS * GROUPS) + (h * GROUPS + g + 1))
                    nc.vector.tensor_copy(pt[p][:, h, g * BLOCKS:(g + 1) * BLOCKS, :].rearrange("p m n -> p (m n)"),
                                          blocks[:, (g % 2) * BANK:(g % 2 + 1) * BANK]).then_inc(pt_dve, 1)

                def divide(i):
                    dve.wait_ge(av_done, i * GROUPS + GROUPS)
                    dve.wait_ge(inv_t_done, i + 1)
                    if not (static(i) and i == 0):
                        dve.wait_ge(projected, i)
                    nc.vector.tensor_tensor(o_t[:], av[:, 0:P], inv_t[:], ALU.mult).then_inc(o_done, 1)

                def invert(i, p):
                    dve.wait_ge(prob_done, i * HEADS + HEADS)
                    nc.vector.reciprocal(inv_sum[:], row_sum[p][:]).then_inc(inv_done, 1)
                    dve.wait_ge(inv_done, i + 1)
                    if not (static(i) and i == 0):
                        dve.wait_ge(wide_turned, i)
                    nc.vector.tensor_copy(inv_wide[:], inv_sum[:].unsqueeze(2).broadcast_to([P, HEADS, HD])).then_inc(wide_done, 1)

                def add_residual(i, p):
                    dve.wait_ge(projected, i + 1)
                    dve.wait_ge(res_done, i + 1)
                    nc.vector.tensor_tensor(z[:], misc[:, P:2 * P], res[p][:], ALU.add).then_inc(z_done, 1)

                def moments(i):
                    dve.wait_ge(z_done, i + 1)
                    nc.vector.bn_stats(out=stats[:], in_=z[:]).then_inc(stats_done, 1)

                def gather_moments(i):
                    wait_apart(dve, c, stats_done, i + 1)
                    nc.vector.bn_aggr(out=mean_var[:], in_=stats[:]).then_inc(mv_done, 1)

                def add_eps(i):
                    dve.wait_ge(mv_done, i + 1)
                    nc.vector.tensor_scalar(var_eps[:], mean_var[:, 1:2], EPS, None, ALU.add).then_inc(eps_done, 1)

                def norm(i, p):
                    add_residual(i, p)
                    moments(i)
                    gather_moments(i)
                    add_eps(i)

                def finish_norm(i, p, n):
                    dve.wait_ge(rstd_done, i + 1)
                    if not (static(i) and i < 2):
                        dve.wait_ge(out_stored[p], 16 * (n - 1))
                    nc.vector.tensor_scalar(normed[p][:], z[:], mean_var[:, 0:1], rstd[:], ALU.subtract,
                                            ALU.mult).then_inc(normed_done, 1)

                def step(i, p, g):
                    for h in range(HEADS):
                        mine = [k for k in range(GROUPS) if COPIES[h][k] == "D"]
                        ahead = (i, p, h + 2, g + 1) if h < 2 else (i + 1, 1 - p, h - 2, g + 1 + p)
                        copy_blocks(i, p, h, mine[0])
                        if h == 0:
                            if not (static(i) and i < 2):
                                divide(i - 2)
                            if not (static(i) and i == 0):
                                invert(i - 1, 1 - p)
                        behind = not (static(i) and i < 2)
                        if behind and h == 2:
                            add_residual(i - 2, p)
                        if behind and h == 3:
                            gather_moments(i - 2)
                        more = not (static(i) and i == TILES - 1 and h >= 2)
                        if more:
                            masked(*ahead[:3], 0, ahead[3])
                        if behind and h == 2:
                            moments(i - 2)
                        if behind and h == 3:
                            add_eps(i - 2)
                        for k in mine[1:]:
                            copy_blocks(i, p, h, k)
                        if more:
                            masked(*ahead[:3], 1, ahead[3])
                            negate(ahead[0], ahead[2])
                        if behind and h == 3:
                            finish_norm(i - 2, p, g)

                for h in range(2):
                    for half in range(2):
                        masked(0, 0, h, half, 1)
                    negate(0, h)
                for i in range(4):
                    step(i, i % 2, i // 2)
                with dve.Fori(2, TILES // 2 - 1) as g:
                    for p in range(2):
                        step(g * 2 + p, p, g)
                step(TILES - 2, 0, TILES // 2 - 1)
                step(TILES - 1, 1, TILES // 2 - 1)
                divide(TILES - 2)
                invert(TILES - 1, 1)
                norm(TILES - 2, 0)
                finish_norm(TILES - 2, 0, TILES // 2)
                divide(TILES - 1)
                norm(TILES - 1, 1)
                finish_norm(TILES - 1, 1, TILES // 2)


def program(nc, io, out):
    with ExitStack() as hold:
        dram = scratch(nc)
        c = constants(nc, hold, io)
        layer0(nc, io, dram, c, 1, "l0")
        general = nc.values_load(c["general"][0:1, 0:1], min_val=0, max_val=1)
        with nc.If(general > 0):
            layer0(nc, io, dram, c, KINDS, "l0g")
        layer1(nc, dram, c, out)


def layout(inputs):
    import numpy as np
    f = {k: np.asarray(v) for k, v in inputs.items()}
    w = f["L1_gnn_in_proj_w"]
    bias = f["L1_gnn_in_proj_b"]
    return {
        "x": np.ascontiguousarray(f["x"]),
        "adj": np.ascontiguousarray(f["adj"]),
        "a": np.ascontiguousarray(np.stack([f[f"L0_gnn_a_{k}"] for k in range(KINDS)], axis=1)),
        "w_qkv": np.ascontiguousarray(w.T),
        "w_out": np.ascontiguousarray(f["L1_gnn_out_w"].T),
        "b_qk": np.ascontiguousarray(bias[:2 * D].reshape(2, D).T),
        "b_v": np.ascontiguousarray(np.broadcast_to(bias[2 * D:], (P, D))),
        "b_out": np.ascontiguousarray(np.broadcast_to(f["L1_gnn_out_b"], (P, D))),
    }


_SHAPES = ("x", "adj", "a", "w_qkv", "w_out", "b_qk", "b_v", "b_out")


def kernel(x, adj, L0_gnn_a_0, L0_gnn_a_1, L0_gnn_a_2, L0_gnn_a_3, L1_gnn_in_proj_w, L1_gnn_in_proj_b,
           L1_gnn_out_w, L1_gnn_out_b):
    import concourse.bacc as bacc
    from concourse.bass_utils import run_bass_kernel_spmd

    arrays = layout(dict(
        x=x, adj=adj, L0_gnn_a_0=L0_gnn_a_0, L0_gnn_a_1=L0_gnn_a_1, L0_gnn_a_2=L0_gnn_a_2, L0_gnn_a_3=L0_gnn_a_3,
        L1_gnn_in_proj_w=L1_gnn_in_proj_w, L1_gnn_in_proj_b=L1_gnn_in_proj_b, L1_gnn_out_w=L1_gnn_out_w,
        L1_gnn_out_b=L1_gnn_out_b))
    nc = bacc.Bacc("TRN2", target_bir_lowering=False, num_devices=1)
    io = {n: nc.dram_tensor(n, list(arrays[n].shape), mybir.dt.from_np(arrays[n].dtype), kind="ExternalInput").ap()
          for n in _SHAPES}
    out = nc.dram_tensor("out", [B, N, D], F32, kind="ExternalOutput").ap()
    program(nc, io, out)
    return run_bass_kernel_spmd(nc, [arrays], core_ids=[0]).results[0]["out"]
```

```python
import concourse.bass as bass
from concourse import mybir
from contextlib import ExitStack

F32 = mybir.dt.float32
F32R = mybir.dt.float32r
BF16 = mybir.dt.bfloat16
I32 = mybir.dt.int32
ACT = mybir.ActivationFunctionType
ALU = mybir.AluOpType

B, N, D = 8, 2048, 128
HEADS, HD = 4, 32
P = 128
NT = N // P
TILES = B * NT
BANK = 512
HALF = N // 2
GROUPS = N // BANK
BLOCKS = BANK // P
KINDS = 4
LEAKY = 0.2
EPS = 1e-5
MASKED0 = -9.0e15 / LEAKY
MASKED1 = -1.0e9
STACK = 3 * HD
Q_SCALE = float(HD) ** -0.5


def wait_apart(engine, c, sem, value):
    if not isinstance(value, int):
        spare = c["spare", engine.engine]
        engine.reg_mov(spare, engine.to_reg(value))
        value = spare
    engine.wait_ge(c["made"], 2)
    engine.wait_ge(sem, value)


def scratch(nc):
    def dram(name, shape, dt):
        return nc.dram_tensor(f"kept_{name}", shape, dt, kind="Internal").ap()
    return dict(
        xt=dram("xt", [B + 2, D, 2 + 2 * KINDS, N], F32),
        x1v=dram("x1v", [TILES, P, 2, D], F32),
        stacks=dram("stacks", [TILES, 3, 2, D, P], F32),
        mask1=dram("mask1", [NT, P, N], BF16),
    )


def constants(nc, hold, io):
    def sb(name, shape, dt=F32):
        return hold.enter_context(nc.sbuf_tensor(f"c_{name}", shape, dt))
    c = dict(
        ident=sb("ident", [P, P]), a=sb("a", [D, KINDS]), w_qkv=sb("w_qkv", [D, 3 * D]), w_out=sb("w_out", [D, D]),
        b_qk=sb("b_qk", [D, 2]), b_q=sb("b_q", [D, 1]), b_v=sb("b_v", [P, D]), b_out=sb("b_out", [P, D]),
        half=sb("half", [P, 1]), minus1=sb("minus1", [P, 1]), high=sb("high", [P, 1]), ones=sb("ones", [P, 1]),
        general=sb("general", [1, 1], I32),
    )
    loaded = hold.enter_context(nc.semaphore("loaded"))
    made = c["made"] = hold.enter_context(nc.semaphore("made"))
    scaled = hold.enter_context(nc.semaphore("scaled"))
    for engine in (nc.vector, nc.gpsimd):
        c["spare", engine.engine] = engine.alloc_register("spare")
    with nc.Block() as block:
        @block.vector
        def _(dve):
            dve.reg_mov(c["spare", dve.engine], 0)

        @block.sync
        def _(sp):
            for dst, src in (("a", "a"), ("w_qkv", "w_qkv"), ("w_out", "w_out"), ("b_qk", "b_qk"),
                             ("b_v", "b_v"), ("b_out", "b_out")):
                sp.dma_start(c[dst][:], io[src]).then_inc(loaded, 16)
            sp.wait_ge(loaded, 6 * 16)
            sp.wait_ge(scaled, 1)

        @block.gpsimd
        def _(pool):
            pool.memset(c["ident"][:], 0.0).then_inc(made, 1)
            pool.memset(c["half"][:], -0.5)
            pool.memset(c["minus1"][:], -1.0)
            pool.memset(c["high"][:], 0.0)
            pool.memset(c["ones"][:], 1.0)
            pool.wait_ge(made, 1)
            pool.affine_select(out=c["ident"][:], in_=c["ident"][:], compare_op=ALU.not_equal, fill=1.0,
                               base=0, pattern=[[-1, P]], channel_multiplier=1).then_inc(made, 1)
            pool.wait_ge(made, 2)

        @block.scalar
        def _(act):
            act.wait_ge(loaded, 6 * 16)
            nc.scalar.mul(c["b_q"][:], c["b_qk"][:, 0:1], Q_SCALE).then_inc(scaled, 1)
    return c


def layer0(nc, io, dram, c, kinds, tag):
    with ExitStack() as hold:
        def sb(name, shape, dt=F32):
            return hold.enter_context(nc.sbuf_tensor(f"{tag}_{name}_", shape, dt))

        def ps(name, cols):
            return hold.enter_context(nc.psum_tensor(f"{tag}_{name}_", [P, cols], F32))

        def sem(name):
            return hold.enter_context(nc.semaphore(f"{tag}_{name}_"))

        def pair(f, name, *rest):
            return [f(f"{name}_{p}", *rest) for p in range(2)]

        first = kinds == 1
        PARTS = 2 + 2 * kinds
        LOT = BLOCKS
        LOTS = NT // LOT + 1
        LOTS_IN = ((LOTS + 1) // 2 * 16, LOTS // 2 * 16)
        LEAD = LOTS * LOT
        x_in = pair(sb, "x_in", [P, D])
        xf = pair(sb, "xf", [D, P])
        ident16 = sb("ident16", [P, P], BF16)
        prep_f = sb("prep_f", [D, kinds, P])
        prep = pair(sb, "prep", [D, PARTS, P], F32R)
        q = pair(sb, "q", [D, 2 * kinds, P], F32R)
        xt = pair(sb, "xt", [D, 2, N], F32R)
        lot_x = pair(sb, "lot_x", [D, LOT * P])
        lot_f = sb("lot_f", [D, kinds, LOT * P])
        lot = pair(sb, "lot", [D, PARTS, LOT * P], F32R)
        xv = pair(sb, "xv", [P, NT, D])
        adj = pair(sb, "adj", [P, N], I32)
        mask = pair(sb, "mask", [P, N], BF16)
        t = pair(sb, "t", [P, N])
        more = sb("more", [P, N]) if kinds > 1 else None
        part_max = pair(sb, "part_max", [P, 2 * kinds])
        row_max = pair(sb, "row_max", [P, 1])
        neg_max = pair(sb, "neg_max", [P, 1])
        row_sum = pair(sb, "row_sum", [P, 1])
        pt = sb("pt", [P, NT, P])
        x_res = pair(sb, "x_res", [P, D])
        inv_sum = sb("inv_sum", [P, 1])
        y = sb("y", [P, D])
        stats = sb("stats", [P, nc.vector.BN_STATS_DIM])
        mean_var = sb("mean_var", [P, 2])
        var_eps = sb("var_eps", [P, 1])
        rstd = sb("rstd", [P, 1])
        x1v = pair(sb, "x1v", [P, 2, D])
        x1t = sb("x1t", [D, P])
        qk_f = sb("qk_f", [D, 2, P])
        qk = pair(sb, "qk", [D, 4, P], F32R)
        junk = sb("junk", [P, N], BF16)
        above = pair(sb, "above", [P, 1])
        mask1 = sb("mask1", [P, N], BF16) if first else None

        scores = ps("scores", N)
        blocks = ps("blocks", 2 * BANK)
        av = ps("av", BANK)
        misc = ps("misc", BANK)

        x_loaded, q_loaded = pair(sem, "x_loaded"), pair(sem, "q_loaded")
        adj_loaded, res_loaded = pair(sem, "adj_loaded"), pair(sem, "res_loaded")
        graph_loaded = pair(sem, "graph_loaded")
        lot_loaded = [sem(f"lot_loaded{j}") for j in range(LOTS)]
        lot_turned, lot_copied, lot_scaled, lot_done = (sem(s) for s in (
            "lot_turned", "lot_copied", "lot_scaled", "lot_done"))
        prep_stored, tail_stored = pair(sem, "prep_stored"), pair(sem, "tail_stored")
        x_turned, x_copied, prep_f_done, prep_hi, prep_done = (sem(s) for s in (
            "x_turned", "x_copied", "prep_f_done", "prep_hi", "prep_done"))
        scored, slope_done, mask_done, part_done, neg_max_done, prob_done = (sem(s) for s in (
            "scored", "slope_done", "mask_done", "part_done", "neg_max_done", "prob_done"))
        if not first:
            merged, row_max_done = sem("merged"), sem("row_max_done")
        turned, pt_act, pt_dve, av_done = (sem(s) for s in ("turned", "pt_act", "pt_dve", "av_done"))
        inv_done, y_done, stats_done, mv_done, eps_done, rstd_done, x1_done = (sem(s) for s in (
            "inv_done", "y_done", "stats_done", "mv_done", "eps_done", "rstd_done", "x1_done"))
        x1_turned, x1t_done, projected, qk_f_done, v_done, qk_hi, qk_done = (sem(s) for s in (
            "x1_turned", "x1t_done", "projected", "qk_f_done", "v_done", "qk_hi", "qk_done"))
        ident16_done = sem("ident16_done")
        if first:
            noted, high_done, mask1_done, mask1_stored, note_summed, note_done = (sem(s) for s in (
                "noted", "high_done", "mask1_done", "mask1_stored", "note_summed", "note_done"))

        ACT_GROUPS, DVE_GROUPS = (0, 1, 3), (2,)
        TAIL_STORES = 4
        LAG = 3

        x_tiles = io["x"].rearrange("b (t p) d -> (b t) p d", p=P)
        adj_tiles = io["adj"].rearrange("b (t p) m -> (b t) p m", p=P)

        def mask_of(k, p):
            return p if kinds == 1 else k % 2

        def row(ap, i):
            return ap[i] if isinstance(i, int) else ap[bass.ds(i, 1)].rearrange("a p d -> (a p) d")

        def xt_part(j, lo, hi):
            if isinstance(j, int):
                return dram["xt"][j // NT, :, lo:hi, j % NT * P:j % NT * P + P]
            return dram["xt"][bass.ds(j // NT, 1), :, lo:hi, bass.ds((j % NT) * P, P)].rearrange("a d k n -> (a d) k n")

        with nc.Block() as block:
            @block.sync
            def _(sp):
                spares = [sp.alloc_register(f"{tag}_spare{k}") for k in range(3)]

                def ahead(*values):
                    for spare, value in zip(spares, values):
                        if not isinstance(value, int):
                            sp.reg_mov(spare, sp.to_reg(value))
                    return [value if isinstance(value, int) else spare for spare, value in zip(spares, values)]

                def store_prep(j, p):
                    sp.wait_ge(prep_done, j + (1 - LEAD))
                    sp.dma_start(xt_part(j, 0, PARTS), prep[p][:].bitcast(F32)).then_inc(prep_stored[p], 16)

                def load_adj(i, p):
                    if not (isinstance(i, int) and i < 2):
                        sp.wait_ge(mask_done, (i - 1) * kinds)
                        if first:
                            sp.wait_ge(noted, i - 1)
                    sp.dma_start(adj[p][:], row(adj_tiles, i)).then_inc(adj_loaded[p], 16)

                def load_q(i, p, n, lot=False):
                    stored, read = ahead(n * 16 + (LOTS_IN[p] - LEAD // 2 * 16), (i - 1) * (2 * kinds))
                    if not lot:
                        sp.wait_ge(prep_stored[p], stored)
                    if not (isinstance(i, int) and i < 2):
                        sp.wait_ge(scored, read)
                    sp.dma_start(q[p][:].bitcast(F32), xt_part(i, 2, PARTS)).then_inc(q_loaded[p], 16)

                def load_xt(b, buf, quarter):
                    stored0, stored1, free = ahead(*(
                        b * (NT // 2 * 16) + (LOTS_IN[p] + ((quarter + 1) * BLOCKS - LEAD) // 2 * 16) for p in range(2)),
                        (b - 1) * (NT * 2 * kinds))
                    sp.wait_ge(prep_stored[0], stored0)
                    sp.wait_ge(prep_stored[1], stored1)
                    if not (isinstance(b, int) and b == 1):
                        sp.wait_ge(scored, free)
                    cols = slice(quarter * BANK, (quarter + 1) * BANK)
                    src = dram["xt"][b, :, 0:2, cols] if isinstance(b, int) else \
                        dram["xt"][bass.ds(b, 1), :, 0:2, cols].rearrange("a d k n -> (a d) k n")
                    sp.dma_start(xt[buf][:, :, cols].bitcast(F32), src).then_inc(graph_loaded[buf], 16)

                def load_xv(b, buf, quarter):
                    if not (isinstance(b, int) and b == 1):
                        sp.wait_ge(av_done, (b - 1) * (NT * GROUPS))
                    begin = b * NT + quarter * BLOCKS
                    src = x_tiles[begin:begin + BLOCKS] if isinstance(b, int) else x_tiles[bass.ds(begin, BLOCKS)]
                    sp.dma_start(xv[buf][:, quarter * BLOCKS:(quarter + 1) * BLOCKS, :],
                                 src.rearrange("t p d -> p t d")).then_inc(graph_loaded[buf], 16)

                def store_mask1(i):
                    sp.wait_ge(mask1_done, i + 1)
                    sp.dma_start(dram["mask1"][i], mask1[:]).then_inc(mask1_stored, 16)

                def store_tail(i, p):
                    sp.wait_ge(x1_done, i + 1)
                    sp.wait_ge(v_done, i + 1)
                    static = isinstance(i, int)
                    sp.dma_start(dram["x1v"][i] if static else
                                 dram["x1v"][bass.ds(i, 1)].rearrange("a p w d -> (a p) w d"),
                                 x1v[p][:]).then_inc(tail_stored[p], 16)
                    sp.wait_ge(qk_done, i + 1)
                    to = dram["stacks"][i] if static else \
                        dram["stacks"][bass.ds(i, 1)].rearrange("a s w d n -> (a s) w d n")
                    for third, (q_part, k_part) in enumerate(((1, 2), (1, 3), (0, 2))):
                        sp.dma_start(to[third].rearrange("w d n -> d w n"),
                                     qk[p][:, q_part:k_part + 1:k_part - q_part, :].bitcast(F32)).then_inc(tail_stored[p], 16)

                def step(b, g, p):
                    i = b * NT + g * 2 + p
                    at = i if isinstance(i, int) else None
                    if at is None or at >= LAG:
                        store_tail(i - LAG, (p - LAG) % 2)
                    if at is None or at < TILES - 2:
                        load_q(i + 2, p, b * (NT // 2) + (g + 2), lot=at is not None and at + 2 < LEAD)
                    if at is None or at >= 2:
                        sp.wait_ge(y_done, i - 1)
                    sp.dma_start(x_res[p][:], row(x_tiles, i)).then_inc(res_loaded[p], 16)
                    if at is None or at >= 2:
                        sp.wait_ge(x_turned, i - 1)
                    sp.dma_start(x_in[p][:], row(x_tiles, (i + LEAD) % TILES)).then_inc(x_loaded[p], 16)
                    if at == 0:
                        load_adj(2, 0)
                    if at is None or at < TILES - 3:
                        load_adj(i + 3, 1 - p)
                    if at != 0:
                        store_prep(i + (LEAD - 1), 1 - p)
                    if first and at is not None and at < NT - 1:
                        store_mask1(at + 1)

                def graph(b, buf, last=False):
                    step(b, 0, 0)
                    step(b, 0, 1)
                    late = NT // 2 - 3
                    if isinstance(b, int) and b == 0:
                        for g in range(1, late):
                            for p in range(2):
                                step(b, g, p)
                    else:
                        with sp.Fori(1, late) as g:
                            for p in range(2):
                                step(b, g, p)
                    for g in range(late, NT // 2):
                        for p in range(2):
                            step(b, g, p)
                            quarter = (g - late) * 2 + p
                            if quarter < GROUPS and not last:
                                load_xt(b + 1, 1 - buf, quarter)
                                load_xv(b + 1, 1 - buf, quarter)

                for j in range(NT // LOT):
                    tiles = slice(j * LOT, (j + 1) * LOT)
                    sp.dma_start(xv[0][:, tiles, :], x_tiles[tiles].rearrange("t p d -> p t d")).then_inc(lot_loaded[j], 16)
                sp.dma_start(t[1][:, 0:LOT * P].rearrange("p (t d) -> p t d", d=D),
                             x_tiles[NT:NT + LOT].rearrange("t p d -> p t d")).then_inc(lot_loaded[-1], 16)
                load_adj(0, 0)
                for j in range(LOTS):
                    b, at = divmod(j * LOT * P, N)
                    sp.wait_ge(lot_done, (j + 1) * (1 + kinds))
                    parts = slice(2 if b == 0 else 0, PARTS)
                    sp.dma_start(dram["xt"][b, :, parts, at:at + LOT * P],
                                 lot[j % 2][:, parts].bitcast(F32)).then_inc(prep_stored[j % 2], 16)
                    if j == 0:
                        sp.wait_ge(prep_stored[0], 16)
                        load_q(0, 0, 1, lot=True)
                        load_q(1, 1, 1, lot=True)
                    if j == 1:
                        load_adj(1, 1)
                if first:
                    store_mask1(0)
                for p in range(2):
                    sp.wait_ge(prep_stored[p], LOTS_IN[p])

                graph(0, 0)
                with sp.Fori(0, B // 2 - 1) as pair_of:
                    for buf in range(2):
                        graph(pair_of * 2 + (1 + buf), 1 - buf)
                graph(B - 1, 1, last=True)
                for i in range(TILES - LAG, TILES):
                    store_tail(i, i % 2)
                for p in range(2):
                    sp.wait_ge(tail_stored[p], TILES // 2 * TAIL_STORES * 16)
                    sp.wait_ge(x_loaded[p], TILES // 2 * 16)
                    sp.wait_ge(prep_stored[p], LOTS_IN[p] + (TILES // 2 - p) * 16)
                if first:
                    sp.wait_ge(mask1_stored, NT * 16)

            @block.gpsimd
            def _(pool):
                def split(j, p):
                    if not (isinstance(j, int) and j < 2):
                        pool.wait_ge(prep_stored[p], (j - p) * 8 + LOTS_IN[p])
                    if not (isinstance(j, int) and j == 0):
                        pool.wait_ge(prep_done, j)
                    wait_apart(pool, c, x_copied, j + 1)
                    nc.gpsimd.tensor_copy(prep[p][:, 0, :], xf[p][:])
                    for k in range(kinds):
                        last = nc.gpsimd.tensor_scalar(prep_f[:, k, :], xf[p][:], c["a"][:, k:k + 1], None, ALU.mult)
                    last.then_inc(prep_f_done, 1)
                    pool.wait_ge(prep_f_done, j + 1)
                    nc.gpsimd.tensor_tensor(prep[p][:, 1, :], xf[p][:], prep[p][:, 0, :].bitcast(F32), ALU.subtract)
                    nc.gpsimd.tensor_copy(prep[p][:, 2:2 + kinds, :], prep_f[:]).then_inc(prep_hi, 1)
                    pool.wait_ge(prep_hi, j + 1)
                    nc.gpsimd.tensor_tensor(prep[p][:, 2 + kinds:, :], prep_f[:], prep[p][:, 2:2 + kinds, :].bitcast(F32),
                                            ALU.subtract).then_inc(prep_done, 1)

                def root(i):
                    pool.wait_ge(eps_done, i + 1)
                    nc.gpsimd.tensor_tensor(rstd[:], var_eps[:], c["half"][:], ALU.pow).then_inc(rstd_done, 1)

                def split_qk(i, p, start):
                    if not start:
                        pool.wait_ge(tail_stored[p], tail_count(i, p))
                    wait_apart(pool, c, qk_f_done, 2 * i + 2)
                    nc.gpsimd.tensor_copy(qk[p][:, 1:3, :], qk_f[:]).then_inc(qk_hi, 1)
                    pool.wait_ge(qk_hi, i + 1)
                    nc.gpsimd.tensor_tensor(qk[p][:, 0:4:3, :], qk_f[:], qk[p][:, 1:3, :].bitcast(F32),
                                            ALU.subtract).then_inc(qk_done, 1)

                def tail_count(i, p):
                    return (i - p) * (TAIL_STORES // 2 * 16)

                nc.gpsimd.tensor_copy(ident16[:], c["ident"][:]).then_inc(ident16_done, 1)

                def step(i, p, start):
                    if not start:
                        root(i - 1)
                    split(i, p)
                    if first:
                        pool.wait_ge(noted, i + 1)
                        nc.gpsimd.tensor_tensor(c["high"][:], c["high"][:], above[p][:], ALU.add).then_inc(high_done, 1)
                    if not start:
                        split_qk(i - 1, 1 - p, isinstance(i, int) and i < 3)

                step(0, 0, True)
                step(1, 1, False)
                step(2, 0, False)
                step(3, 1, False)
                with pool.Fori(2, TILES // 2) as g:
                    for p in range(2):
                        step(g * 2 + p, p, False)
                root(TILES - 1)
                split_qk(TILES - 1, 1, False)

            @block.tensor
            def _(pe):
                def turn_x(p, n):
                    pe.wait_ge(x_loaded[p], 16 * n)
                    nc.tensor.transpose(misc[:, 0:P], x_in[p][:], c["ident"][:]).then_inc(x_turned, 1)

                def score(i, p, b, buf, n, parts, start=False):
                    if 0 in parts:
                        pe.wait_ge(q_loaded[p], 16 * n)
                    for part in parts:
                        for k, h in [divmod(part, 2)]:
                            if part == 0 and not (isinstance(b, int) and b == 0):
                                pe.wait_ge(graph_loaded[buf], (b + buf) * (2 * GROUPS * 8))
                            if not (start and k == 0):
                                pe.wait_ge(part_done, i * (2 * kinds) + (2 * k + h - 1))
                            for s, (q_part, x_part) in enumerate(((k, 0), (k, 1), (kinds + k, 0))):
                                for bank in range(2):
                                    at = h * HALF + bank * BANK
                                    nc.tensor.matmul(scores[:, at:at + BANK], q[p][:, q_part, :],
                                                     xt[buf][:, x_part, at:at + BANK], start=(s == 0), stop=False)
                            if h == 0:
                                pe.wait_ge(mask_done, i * kinds + (k + 1))
                            for bank in range(2):
                                at = h * HALF + bank * BANK
                                last = nc.tensor.matmul(scores[:, at:at + BANK], ident16[:], mask[mask_of(k, p)][:, at:at + BANK],
                                                        start=False, stop=True)
                            last.then_inc(scored, 1)

                def turn(i, p, g, start):
                    if g == 0:
                        pe.wait_ge(prob_done, i + 1)
                    if not (start and g < 2):
                        free_of(i, g)
                    for k in range(BLOCKS):
                        m = g * BLOCKS + k
                        last = nc.tensor.transpose(blocks[:, (g % 2) * BANK + k * P:(g % 2) * BANK + (k + 1) * P],
                                                   t[p][:, m * P:(m + 1) * P], c["ident"][:])
                    last.then_inc(turned, 1)

                def free_of(i, g):
                    prev, tile = (g - 2, i) if g >= 2 else (g + 2, i - 1)
                    wait_pt(tile, prev)

                def wait_pt(tile, g):
                    if g in ACT_GROUPS:
                        pe.wait_ge(pt_act, tile * len(ACT_GROUPS) + (ACT_GROUPS.index(g) + 1))
                    else:
                        pe.wait_ge(pt_dve, tile * len(DVE_GROUPS) + (DVE_GROUPS.index(g) + 1))

                def values(i, g, buf, start):
                    if g == 0:
                        if not start:
                            pe.wait_ge(y_done, i)
                    wait_pt(i, g)
                    for k in range(BLOCKS):
                        m = g * BLOCKS + k
                        last = nc.tensor.matmul(av[:, 0:D], pt[:, m, :], xv[buf][:, m, :], start=(m == 0), stop=(m == NT - 1))
                    last.then_inc(av_done, 1)

                def turn_x1(i, p):
                    pe.wait_ge(x1_done, i + 1)
                    pe.wait_ge(x_copied, TILES if isinstance(i, int) and i == TILES - 1 else i + 2)
                    nc.tensor.transpose(misc[:, P:2 * P], x1v[p][:, 0, :], c["ident"][:]).then_inc(x1_turned, 1)

                def project(i):
                    pe.wait_ge(x1t_done, i + 1)
                    for w in range(2):
                        nc.tensor.matmul(misc[:, w * P:(w + 1) * P], c["w_qkv"][:, w * D:(w + 1) * D], x1t[:],
                                         start=True, stop=True)
                    nc.tensor.matmul(misc[:, 2 * P:3 * P], x1t[:], c["w_qkv"][:, 2 * D:3 * D],
                                     start=True, stop=True).then_inc(projected, 1)

                for j in range(LOTS):
                    pe.wait_ge(lot_loaded[j], 16)
                    if j:
                        pe.wait_ge(lot_copied, 2 * j - 1)
                    for k in range(LOT):
                        tile = xv[0][:, j * LOT + k, :] if j < GROUPS else t[1][:, k * P:(k + 1) * P]
                        last = nc.tensor.transpose(misc[:, k * P:(k + 1) * P], tile, c["ident"][:])
                    last.then_inc(lot_turned, 1)
                pe.wait_ge(ident16_done, 1)
                pe.wait_ge(lot_done, NT // LOT * (1 + kinds))
                score(0, 0, 0, 0, 1, range(2 * kinds), start=True)

                def step(b, buf, g, p, following, start=False, end=False):
                    i = b * NT + g * 2 + p
                    n = b * (NT // 2) + g + 1
                    early, late = (range(1), range(1, 2)) if kinds == 1 else ((), range(2 * kinds))
                    if not end:
                        score(i + 1, 1 - p, *following, n + p, early)
                    if start:
                        pe.wait_ge(lot_copied, 2 * LOTS)
                    elif not (isinstance(i, int) and i < 2):
                        pe.wait_ge(qk_f_done, 2 * (i - 1))
                        pe.wait_ge(v_done, i - 1)
                    turn_x(p, n)
                    turn(i, p, 0, start)
                    turn(i, p, 1, start)
                    if not end:
                        score(i + 1, 1 - p, *following, n + p, late)
                    if not start:
                        turn_x1(i - 1, 1 - p)
                    turn(i, p, 2, start)
                    values(i, 0, buf, start)
                    turn(i, p, 3, start)
                    values(i, 1, buf, start)
                    if not start:
                        project(i - 1)
                    values(i, 2, buf, start)
                    values(i, 3, buf, start)

                def graph(b, buf, begin=0, last=False):
                    with pe.Fori(begin, NT // 2 - 1) as g:
                        for p in range(2):
                            step(b, buf, g, p, (b, buf))
                    step(b, buf, NT // 2 - 1, 0, (b, buf))
                    step(b, buf, NT // 2 - 1, 1, (b + 1, 1 - buf), end=last)

                step(0, 0, 0, 0, (0, 0), start=True)
                step(0, 0, 0, 1, (0, 0))
                graph(0, 0, begin=1)
                with pe.Fori(0, B // 2 - 1) as two:
                    graph(two * 2 + 1, 1)
                    graph(two * 2 + 2, 0)
                graph(B - 1, 1, last=True)
                pe.wait_ge(qk_f_done, 2 * (TILES - 1))
                pe.wait_ge(v_done, TILES - 1)
                turn_x1(TILES - 1, 1)
                project(TILES - 1)
                if first:
                    pe.wait_ge(high_done, TILES)
                    nc.tensor.matmul(av[0:1, 0:1], c["high"][:], c["ones"][:], start=True, stop=True).then_inc(note_summed, 1)

            @block.scalar
            def _(act):
                def slope(i, p, start, parts=range(2 * kinds)):
                    if not start and 0 in parts:
                        act.wait_ge(turned, (i - 1) * GROUPS)
                    for part in parts:
                        k, h = divmod(part, 2)
                        act.wait_ge(scored, i * (2 * kinds) + (part + 1))
                        dst = more if k else t[p]
                        if k and not (isinstance(i, int) and i == 0 and k == 1):
                            act.wait_ge(merged, i * (2 * (kinds - 1)) + (2 * (k - 1) + h - 1))
                        nc.scalar.activation(dst[:, h * HALF:(h + 1) * HALF], scores[:, h * HALF:(h + 1) * HALF],
                                             ACT.Relu, scale=1.0 / LEAKY - 1.0).then_inc(slope_done, 1)

                def copy_blocks(i, g):
                    act.wait_ge(turned, i * GROUPS + (g + 1))
                    nc.scalar.activation(pt[:, g * BLOCKS:(g + 1) * BLOCKS, :].rearrange("p m n -> p (m n)"),
                                         blocks[:, (g % 2) * BANK:(g % 2 + 1) * BANK], ACT.Copy).then_inc(pt_act, 1)

                def probabilities(i, p, start):
                    act.wait_ge(neg_max_done, i + 1)
                    if not start:
                        act.wait_ge(inv_done, i - 1)
                    nc.scalar.activation(t[p][:], t[p][:], ACT.Exp, bias=neg_max[p][:],
                                         accum_out=row_sum[p][:]).then_inc(prob_done, 1)

                def note(i, p, n, start):
                    act.wait_ge(adj_loaded[p], 16 * n)
                    if not start:
                        act.wait_ge(high_done, i - 1)
                    if not (isinstance(i, int) and i == 0):
                        act.wait_ge(noted, i)
                    nc.scalar.activation(junk[:], adj[p][:], ACT.Relu, bias=c["minus1"][:],
                                         accum_out=above[p][:]).then_inc(noted, 1)

                def qk_bias(i, start):
                    act.wait_ge(projected, i + 1)
                    if not start:
                        act.wait_ge(qk_done, i)
                    nc.scalar.activation(qk_f[:, 0, :], misc[:, 0:P], ACT.Identity, bias=c["b_q"][:],
                                         scale=Q_SCALE).then_inc(qk_f_done, 1)
                    nc.scalar.activation(qk_f[:, 1, :], misc[:, P:2 * P], ACT.Identity,
                                         bias=c["b_qk"][:, 1:2]).then_inc(qk_f_done, 1)

                def scale_lot(j):
                    act.wait_ge(lot_copied, 2 * j + 1)
                    if j:
                        act.wait_ge(lot_done, j * (1 + kinds))
                    if j >= 2:
                        act.wait_ge(prep_stored[j % 2], j // 2 * 16)
                    for k in range(kinds):
                        nc.scalar.activation(lot_f[:, k, :], lot_x[j % 2][:], ACT.Copy, scale=c["a"][:, k:k + 1]).then_inc(lot_scaled, 1)
                    for k in range(kinds):
                        act.wait_ge(lot_scaled, j * (2 * kinds) + (k + 1))
                        nc.scalar.activation(lot[j % 2][:, 2 + k, :], lot_f[:, k, :], ACT.Copy).then_inc(lot_scaled, 1)

                for j in range(LOTS):
                    scale_lot(j)
                slope(0, 0, True)
                probabilities(0, 0, True)
                if first:
                    note(0, 0, 1, True)
                    note(1, 1, 1, True)

                def step(i, p, g, start, end=False):
                    early, late = (range(1), range(1, 2)) if kinds == 1 else ((), range(2 * kinds))
                    if not end:
                        slope(i + 1, 1 - p, start, early)
                    for k in ACT_GROUPS[:-1]:
                        copy_blocks(i, k)
                    if not end:
                        slope(i + 1, 1 - p, start, late)
                    copy_blocks(i, ACT_GROUPS[-1])
                    if not end:
                        probabilities(i + 1, 1 - p, start)
                    if not start:
                        qk_bias(i - 1, isinstance(i, int) and i == 1)
                    if first and not (isinstance(i, int) and i >= TILES - 2):
                        note(i + 2, p, g + 2, False)

                step(0, 0, 0, True)
                step(1, 1, 0, False)
                with act.Fori(1, TILES // 2 - 1) as g:
                    for p in range(2):
                        step(g * 2 + p, p, g, False)
                g = TILES // 2 - 1
                step(2 * g, 0, g, False)
                step(2 * g + 1, 1, g, False, end=True)
                qk_bias(TILES - 1, False)

            @block.vector
            def _(dve):
                def copy_x(j, p):
                    dve.wait_ge(x_turned, j + 1)
                    if not (isinstance(j, int) and j < 2):
                        dve.wait_ge(prep_done, j - 1)
                    nc.vector.tensor_copy(xf[p][:], misc[:, 0:P]).then_inc(x_copied, 1)

                def make_mask(i, k, p, n, start, make1=False):
                    if k == 0:
                        dve.wait_ge(adj_loaded[p], 16 * n)
                    if make1:
                        if not (isinstance(i, int) and i == 0):
                            dve.wait_ge(mask1_stored, i * 16)
                        nc.vector.tensor_scalar(mask1[:], adj[p][:], 0.0, MASKED1, ALU.is_equal,
                                                ALU.mult).then_inc(mask1_done, 1)
                    if not start:
                        dve.wait_ge(scored, (i * kinds + k - 1) * 2)
                    nc.vector.tensor_scalar(mask[mask_of(k, p)][:], adj[p][:], float(k + 1), MASKED0, ALU.not_equal,
                                            ALU.mult).then_inc(mask_done, 1)

                def masked_max(i, p, n, start, parts=range(2 * kinds)):
                    for part in parts:
                        k, h = divmod(part, 2)
                        if kinds > 1 and part == 0:
                            make_mask(i, 0, p, n, start)
                        if h == 0 and 1 <= k + 1 < kinds:
                            make_mask(i, k + 1, p, n, start and k + 1 < 2)
                        dst = more if k else t[p]
                        wait_apart(dve, c, slope_done, i * (2 * kinds) + (part + 1))
                        cols = slice(h * HALF, (h + 1) * HALF)
                        nc.vector.tensor_tensor_reduce(
                            out=dst[:, cols], in0=scores[:, cols], in1=dst[:, cols], scale=LEAKY, scalar=-3.0e38,
                            op0=ALU.add, op1=ALU.max, accum_out=part_max[p][:, part:part + 1]).then_inc(part_done, 1)
                        if k:
                            dve.wait_ge(part_done, i * (2 * kinds) + (part + 1))
                            nc.vector.tensor_tensor(t[p][:, cols], t[p][:, cols], more[:, cols],
                                                    ALU.max).then_inc(merged, 1)
                    if 2 * kinds - 1 not in parts:
                        return
                    dve.wait_ge(part_done, i * (2 * kinds) + (2 * kinds))
                    if kinds > 1:
                        nc.vector.reduce_max(row_max[p][:], part_max[p][:], axis=mybir.AxisListType.X).then_inc(row_max_done, 1)
                        dve.wait_ge(row_max_done, i + 1)
                        nc.vector.tensor_scalar(neg_max[p][:], row_max[p][:], -1.0, None, ALU.mult).then_inc(neg_max_done, 1)
                    else:
                        nc.vector.tensor_scalar(neg_max[p][:], part_max[p][:, 0:1], part_max[p][:, 1:2], -1.0,
                                                ALU.max, ALU.mult).then_inc(neg_max_done, 1)

                def copy_blocks(i, g):
                    dve.wait_ge(turned, i * GROUPS + (g + 1))
                    nc.vector.tensor_copy(pt[:, g * BLOCKS:(g + 1) * BLOCKS, :].rearrange("p m n -> p (m n)"),
                                          blocks[:, (g % 2) * BANK:(g % 2 + 1) * BANK]).then_inc(pt_dve, 1)

                def norm(i, p, n, start):
                    dve.wait_ge(prob_done, i + 1)
                    nc.vector.reciprocal(inv_sum[:], row_sum[p][:]).then_inc(inv_done, 1)
                    dve.wait_ge(inv_done, i + 1)
                    dve.wait_ge(res_loaded[p], 16 * n)
                    dve.wait_ge(av_done, (i + 1) * GROUPS)
                    nc.vector.scalar_tensor_tensor(out=y[:], in0=av[:, 0:D], scalar=inv_sum[:], in1=x_res[p][:],
                                                   op0=ALU.mult, op1=ALU.add).then_inc(y_done, 1)
                    dve.wait_ge(y_done, i + 1)
                    nc.vector.bn_stats(out=stats[:], in_=y[:]).then_inc(stats_done, 1)
                    wait_apart(dve, c, stats_done, i + 1)
                    nc.vector.bn_aggr(out=mean_var[:], in_=stats[:]).then_inc(mv_done, 1)
                    dve.wait_ge(mv_done, i + 1)
                    nc.vector.tensor_scalar(var_eps[:], mean_var[:, 1:2], EPS, None, ALU.add).then_inc(eps_done, 1)

                def finish_norm(i, p, start):
                    dve.wait_ge(rstd_done, i + 1)
                    if not start:
                        dve.wait_ge(tail_stored[p], (i - p) * (TAIL_STORES // 2 * 16))
                    nc.vector.tensor_scalar(x1v[p][:, 0, :], y[:], mean_var[:, 0:1], rstd[:], ALU.subtract,
                                            ALU.mult).then_inc(x1_done, 1)

                def copy_x1t(i):
                    dve.wait_ge(x1_turned, i + 1)
                    nc.vector.tensor_copy(x1t[:], misc[:, P:2 * P]).then_inc(x1t_done, 1)

                def v_bias(i, p):
                    dve.wait_ge(projected, i + 1)
                    dve.wait_ge(qk_f_done, 2 * (i + 1))
                    nc.vector.tensor_tensor(x1v[p][:, 1, :], misc[:, 2 * P:3 * P], c["b_v"][:], ALU.add).then_inc(v_done, 1)

                def split_lot(j):
                    if j < NT // LOT:
                        hi, lo = (xt[0][:, part, j * LOT * P:(j + 1) * LOT * P] for part in range(2))
                    else:
                        hi, lo = (lot[j % 2][:, part, :] for part in range(2))
                    dve.wait_ge(lot_turned, j + 1)
                    nc.vector.tensor_copy(lot_x[j % 2][:], misc[:]).then_inc(lot_copied, 1)
                    dve.wait_ge(lot_copied, 2 * j + 1)
                    nc.vector.tensor_copy(hi, lot_x[j % 2][:]).then_inc(lot_copied, 1)
                    dve.wait_ge(lot_copied, 2 * j + 2)
                    nc.vector.tensor_tensor(lo, lot_x[j % 2][:], hi.bitcast(F32), ALU.subtract).then_inc(lot_done, 1)
                    for k in range(kinds):
                        dve.wait_ge(lot_scaled, j * (2 * kinds) + (kinds + k + 1))
                        nc.vector.tensor_tensor(lot[j % 2][:, 2 + kinds + k, :], lot_f[:, k, :],
                                                lot[j % 2][:, 2 + k, :].bitcast(F32), ALU.subtract).then_inc(lot_done, 1)

                for j in range(NT // LOT):
                    split_lot(j)
                if kinds == 1:
                    make_mask(0, 0, 0, 1, True, make1=True)
                split_lot(NT // LOT)
                masked_max(0, 0, 1, True)
                if kinds == 1:
                    make_mask(1, 0, 1, 1, True, make1=True)

                def step(i, p, g, start, end=False, make1=False):
                    if not start:
                        norm(i - 1, 1 - p, g + p, False)
                    copy_x(i, p)
                    if not start:
                        finish_norm(i - 1, 1 - p, isinstance(i, int) and i < 3)
                    early, late = (range(1), range(1, 2)) if kinds == 1 else (range(2 * kinds), ())
                    if not end:
                        masked_max(i + 1, 1 - p, g + 1 + p, isinstance(i, int) and i == 0, early)
                    if not start:
                        copy_x1t(i - 1)
                    if not end:
                        masked_max(i + 1, 1 - p, g + 1 + p, isinstance(i, int) and i == 0, late)
                    for k in DVE_GROUPS:
                        copy_blocks(i, k)
                    if kinds == 1 and not (isinstance(i, int) and i >= TILES - 2):
                        make_mask(i + 2, 0, p, g + 2, False, make1)
                    if not start:
                        v_bias(i - 1, 1 - p)

                step(0, 0, 0, True, make1=first)
                step(1, 1, 0, False, make1=first)
                step(2, 0, 1, False, make1=first)
                step(3, 1, 1, False, make1=first)
                with dve.Fori(2, NT // 2 - 1) as g:
                    for p in range(2):
                        step(g * 2 + p, p, g, False, make1=first)
                g = NT // 2 - 1
                step(2 * g, 0, g, False)
                step(2 * g + 1, 1, g, False)
                with dve.Fori(NT // 2, TILES // 2 - 1) as g:
                    for p in range(2):
                        step(g * 2 + p, p, g, False)
                g = TILES // 2 - 1
                step(2 * g, 0, g, False)
                step(2 * g + 1, 1, g, False, end=True)
                norm(TILES - 1, 1, TILES // 2, False)
                finish_norm(TILES - 1, 1, False)
                copy_x1t(TILES - 1)
                v_bias(TILES - 1, 1)
                if first:
                    dve.wait_ge(note_summed, 1)
                    nc.vector.tensor_scalar(c["general"][:], av[0:1, 0:1], 0.0, None, ALU.is_gt).then_inc(note_done, 1)
                    dve.wait_ge(note_done, 1)


def layer1(nc, dram, c, out):
    with ExitStack() as hold:
        def sb(name, shape, dt=F32):
            return hold.enter_context(nc.sbuf_tensor(f"l1_{name}_", shape, dt))

        def ps(name, cols):
            return hold.enter_context(nc.psum_tensor(f"l1_{name}_", [P, cols], F32))

        def sem(name):
            return hold.enter_context(nc.semaphore(f"l1_{name}_"))

        def pair(f, name, *rest):
            return [f(f"{name}_{p}", *rest) for p in range(2)]

        q = sb("q", [STACK, HEADS, P], F32R)
        keys = sb("keys", [STACK, HEADS, N], F32R)
        v = sb("v", [P, NT, D])
        mask = pair(sb, "mask", [P, N], BF16)
        t = sb("t", [P, HEADS, N])
        part_max = sb("part_max", [P, HEADS, 2])
        neg_max = sb("neg_max", [P, HEADS])
        row_sum = pair(sb, "row_sum", [P, HEADS])
        pt = pair(sb, "pt", [P, HEADS, NT, P])
        inv_sum = sb("inv_sum", [P, HEADS])
        inv_wide = sb("inv_wide", [P, HEADS, HD])
        inv_t = sb("inv_t", [D, P])
        o_t = sb("o_t", [D, P])
        x1 = pair(sb, "x1", [P, D])
        res = pair(sb, "res", [P, D])
        z = sb("z", [P, D])
        stats = sb("stats", [P, nc.vector.BN_STATS_DIM])
        mean_var = sb("mean_var", [P, 2])
        var_eps = sb("var_eps", [P, 1])
        rstd = sb("rstd", [P, 1])
        normed = pair(sb, "normed", [P, D])

        scores = ps("scores", N)
        blocks = ps("blocks", 2 * BANK)
        av = ps("av", BANK)
        misc = ps("misc", BANK)

        q_loaded = [sem(f"q_loaded{h}") for h in range(HEADS)]
        keys_loaded = [sem(f"keys_loaded{h}") for h in range(HEADS)]
        v_loaded = [sem(f"v_loaded{g}") for g in range(GROUPS)]
        mask_loaded, x1_loaded, out_stored = pair(sem, "mask_loaded"), pair(sem, "x1_loaded"), pair(sem, "out_stored")
        scored, part_done, neg_max_done, prob_done = (sem(s) for s in ("scored", "part_done", "neg_max_done", "prob_done"))
        turned, pt_act, pt_dve, av_done = (sem(s) for s in ("turned", "pt_act", "pt_dve", "av_done"))
        inv_done, wide_done, wide_turned, inv_t_done, o_done = (sem(s) for s in (
            "inv_done", "wide_done", "wide_turned", "inv_t_done", "o_done"))
        projected, res_done, z_done, stats_done, mv_done, eps_done, rstd_done, normed_done = (sem(s) for s in (
            "projected", "res_done", "z_done", "stats_done", "mv_done", "eps_done", "rstd_done", "normed_done"))

        COPIES = ("ADAA",) * HEADS
        LAG = 3

        def copied(i, h, g):
            who = COPIES[h][g]
            before = sum(x.count(who) for x in COPIES[:h]) + COPIES[h][:g + 1].count(who)
            return (pt_act if who == "A" else pt_dve), i * sum(x.count(who) for x in COPIES) + before

        def static(i):
            return isinstance(i, int)

        out_tiles = out.rearrange("b (t p) d -> (b t) p d", p=P)

        def row(ap, i):
            return ap[i] if static(i) else ap[bass.ds(i, 1)].rearrange("a p d -> (a p) d")

        with nc.Block() as block:
            @block.sync
            def _(sp):
                def load_q(i, h):
                    if not (static(i) and i == 0):
                        sp.wait_ge(scored, i * (2 * HEADS) + (2 * h + 2 - 2 * HEADS))
                    for third in range(3):
                        src = dram["stacks"][i, third, 0, h * HD:(h + 1) * HD] if static(i) else \
                            dram["stacks"][bass.ds(i, 1), third, 0, h * HD:(h + 1) * HD].rearrange("a d n -> (a d) n")
                        sp.dma_start(q[third * HD:(third + 1) * HD, h, :].bitcast(F32), src).then_inc(q_loaded[h], 16)

                def load_keys(b, h):
                    for third in range(3):
                        src = dram["stacks"][b * NT:(b + 1) * NT, third, 1, h * HD:(h + 1) * HD] if static(b) else \
                            dram["stacks"][bass.ds(b * NT, NT), third, 1, h * HD:(h + 1) * HD]
                        sp.dma_start(keys[third * HD:(third + 1) * HD, h, :].rearrange("d (t n) -> d t n", n=P).bitcast(F32),
                                     src.rearrange("t d n -> d t n")).then_inc(keys_loaded[h], 16)

                def load_mask(i, p):
                    if not (static(i) and i < 2):
                        sp.wait_ge(part_done, (i - 1) * (2 * HEADS))
                    sp.dma_start(mask[p][:], row(dram["mask1"], i % NT)).then_inc(mask_loaded[p], 16)

                def load_v(b):
                    for g in range(GROUPS):
                        if static(b):
                            src = dram["x1v"][b * NT + g * BLOCKS:b * NT + (g + 1) * BLOCKS, :, 1, :]
                        else:
                            src = dram["x1v"][bass.ds(b * NT + g * BLOCKS, BLOCKS), :, 1, :]
                        if not (static(b) and b == 0):
                            sp.wait_ge(av_done, b * (NT * GROUPS) + (g + 1 - GROUPS))
                        sp.dma_start(v[:, g * BLOCKS:(g + 1) * BLOCKS, :],
                                     src.rearrange("t p d -> p t d")).then_inc(v_loaded[g], 16)

                def load_x1(i, p):
                    if not (static(i) and i < 2):
                        sp.wait_ge(res_done, i - 1)
                    src = dram["x1v"][i, :, 0, :] if static(i) else \
                        dram["x1v"][bass.ds(i, 1), :, 0, :].rearrange("a p d -> (a p) d")
                    sp.dma_start(x1[p][:], src).then_inc(x1_loaded[p], 16)

                def store(i, p):
                    sp.wait_ge(normed_done, i + 1)
                    sp.dma_start(row(out_tiles, i), normed[p][:]).then_inc(out_stored[p], 16)

                def step(b, nt, p, load_after=False, first_of=False):
                    i = b * NT + nt
                    if not (static(i) and i < LAG):
                        store(i - LAG, (p - LAG) % 2)
                    for h in range(HEADS):
                        if not (static(i) and i == TILES - 1):
                            load_q(i + 1, h)
                        if load_after:
                            load_keys(b + 1, h)
                    load_x1(i, p)
                    if not (static(i) and i >= TILES - 2):
                        load_mask(i + 2, p)
                    if first_of and not (static(b) and b == 0):
                        load_v(b)

                def graph(b, last=False):
                    step(b, 0, 0, first_of=True)
                    step(b, 1, 1)
                    if static(b) and b == 0:
                        for nt in range(2, NT - 2):
                            step(b, nt, nt % 2)
                    else:
                        with sp.Fori(1, NT // 2 - 1) as g:
                            for p in range(2):
                                step(b, g * 2 + p, p)
                    step(b, NT - 2, 0)
                    step(b, NT - 1, 1, load_after=not last)

                for h in range(HEADS):
                    load_q(0, h)
                    load_keys(0, h)
                    if h == 0:
                        load_mask(0, 0)
                load_mask(1, 1)
                load_v(0)
                graph(0)
                with sp.Fori(1, B - 1) as b:
                    graph(b)
                graph(B - 1, last=True)
                for i in range(TILES - LAG, TILES):
                    store(i, i % 2)
                for p in range(2):
                    sp.wait_ge(out_stored[p], TILES // 2 * 16)

            @block.gpsimd
            def _(pool):
                def residual(i, p, n):
                    pool.wait_ge(x1_loaded[p], 16 * n)
                    if not (static(i) and i < 2):
                        pool.wait_ge(z_done, i - 1)
                    nc.gpsimd.tensor_tensor(res[p][:], x1[p][:], c["b_out"][:], ALU.add).then_inc(res_done, 1)

                def root(i):
                    pool.wait_ge(eps_done, i + 1)
                    nc.gpsimd.tensor_tensor(rstd[:], var_eps[:], c["half"][:], ALU.pow).then_inc(rstd_done, 1)

                residual(0, 0, 1)
                residual(1, 1, 1)
                with pool.Fori(1, TILES // 2) as g:
                    for p in range(2):
                        residual(g * 2 + p, p, g + 1)
                        root(g * 2 + (p - 2))
                root(TILES - 2)
                root(TILES - 1)

            @block.tensor
            def _(pe):
                def score(i, h, half):
                    if half == 0:
                        pe.wait_ge(q_loaded[h], i * 48 + 48)
                        pe.wait_ge(keys_loaded[h], (i // NT) * 48 + 48)
                    if not (static(i) and i == 0 and h == 0):
                        pe.wait_ge(part_done, i * (2 * HEADS) + (2 * h + half - 1))
                    for bank in range(2):
                        at = half * HALF + bank * BANK
                        last = nc.tensor.matmul(scores[:, at:at + BANK], q[:, h, :], keys[:, h, at:at + BANK],
                                                start=True, stop=True)
                    last.then_inc(scored, 1)

                def turn(i, h, g):
                    if g == 0:
                        pe.wait_ge(prob_done, i * HEADS + (h + 1))
                    if g >= 2:
                        pe.wait_ge(*copied(i, h, g - 2))
                    elif h:
                        pe.wait_ge(*copied(i, h - 1, g + 2))
                    elif not (static(i) and i == 0):
                        pe.wait_ge(*copied(i - 1, HEADS - 1, g + 2))
                    for k in range(BLOCKS):
                        m = g * BLOCKS + k
                        last = nc.tensor.transpose(blocks[:, (g % 2) * BANK + k * P:(g % 2) * BANK + (k + 1) * P],
                                                   t[:, h, m * P:(m + 1) * P], c["ident"][:])
                    last.then_inc(turned, 1)

                def values(i, p, g):
                    if g == 0:
                        if not (static(i) and i == 0):
                            pe.wait_ge(o_done, i)
                        for who in "AD":
                            pe.wait_ge(*copied(i, HEADS - 1, COPIES[-1].rindex(who)))
                    pe.wait_ge(v_loaded[g], (i // NT) * 16 + 16)
                    for k in range(BLOCKS):
                        m = g * BLOCKS + k
                        for h in range(HEADS):
                            lanes = slice(h * HD, (h + 1) * HD)
                            last = nc.tensor.matmul(av[lanes, 0:P], v[:, m, lanes], pt[p][:, h, m, :],
                                                    start=(m == 0), stop=(m == NT - 1))
                    last.then_inc(av_done, 1)

                def turn_wide(i):
                    pe.wait_ge(wide_done, i + 1)
                    if not (static(i) and i < 2):
                        pe.wait_ge(z_done, i - 1)
                    nc.tensor.transpose(misc[:, 0:P], inv_wide[:].rearrange("p h d -> p (h d)"),
                                        c["ident"][:]).then_inc(wide_turned, 1)

                def project(i, last=False):
                    pe.wait_ge(o_done, i + 1)
                    pe.wait_ge(inv_t_done, TILES if last else i + 2)
                    nc.tensor.matmul(misc[:, P:2 * P], o_t[:], c["w_out"][:], start=True, stop=True).then_inc(projected, 1)

                def step(i, p):
                    for h in range(HEADS):
                        ahead = (i, h + 2) if h < 2 else (i + 1, h - 2)
                        more = not (static(i) and i == TILES - 1 and h >= 2)
                        turn(i, h, 0)
                        turn(i, h, 1)
                        if more:
                            score(*ahead, 0)
                        turn(i, h, 2)
                        if more:
                            score(*ahead, 1)
                        turn(i, h, 3)
                        if h == 0 and not (static(i) and i == 0):
                            turn_wide(i - 1)
                        if not (static(i) and i == 0):
                            values(i - 1, 1 - p, h)
                        if h == 1 and not (static(i) and i < 2):
                            project(i - 2)

                for h in range(2):
                    for half in range(2):
                        score(0, h, half)
                for i in range(4):
                    step(i, i % 2)
                with pe.Fori(2, TILES // 2 - 1) as g:
                    for p in range(2):
                        step(g * 2 + p, p)
                step(TILES - 2, 0)
                step(TILES - 1, 1)
                turn_wide(TILES - 1)
                for g in range(GROUPS):
                    values(TILES - 1, 1, g)
                project(TILES - 2)
                pe.wait_ge(z_done, TILES - 1)
                project(TILES - 1, last=True)

            @block.scalar
            def _(act):
                def probabilities(i, p, h):
                    act.wait_ge(neg_max_done, i * HEADS + (h + 1))
                    if h == 0 and not (static(i) and i < 2):
                        act.wait_ge(inv_done, i - 1)
                    nc.scalar.activation(t[:, h, :], t[:, h, :], ACT.Exp, bias=neg_max[:, h:h + 1],
                                         accum_out=row_sum[p][:, h:h + 1]).then_inc(prob_done, 1)

                def copy_blocks(i, p, h, g):
                    act.wait_ge(turned, i * (HEADS * GROUPS) + (h * GROUPS + g + 1))
                    nc.scalar.activation(pt[p][:, h, g * BLOCKS:(g + 1) * BLOCKS, :].rearrange("p m n -> p (m n)"),
                                         blocks[:, (g % 2) * BANK:(g % 2 + 1) * BANK], ACT.Copy).then_inc(pt_act, 1)

                def copy_inv(i):
                    act.wait_ge(wide_turned, i + 1)
                    if not (static(i) and i == 0):
                        act.wait_ge(o_done, i)
                    nc.scalar.activation(inv_t[:], misc[:, 0:P], ACT.Copy).then_inc(inv_t_done, 1)

                def step(i, p):
                    for h in range(HEADS):
                        mine = [g for g in range(GROUPS) if COPIES[h][g] == "A"]
                        if h == 1 and not (static(i) and i == 0):
                            copy_inv(i - 1)
                        copy_blocks(i, p, h, mine[0])
                        if not (static(i) and i == TILES - 1 and h == HEADS - 1):
                            if h < HEADS - 1:
                                probabilities(i, p, h + 1)
                            else:
                                probabilities(i + 1, 1 - p, 0)
                        for g in mine[1:]:
                            copy_blocks(i, p, h, g)

                probabilities(0, 0, 0)
                step(0, 0)
                step(1, 1)
                with act.Fori(1, TILES // 2 - 1) as g:
                    for p in range(2):
                        step(g * 2 + p, p)
                step(TILES - 2, 0)
                step(TILES - 1, 1)
                copy_inv(TILES - 1)

            @block.vector
            def _(dve):
                def masked(i, p, h, half, n):
                    if h == 0 and half == 0:
                        dve.wait_ge(mask_loaded[p], 16 * n)
                    if half == 0 and not (static(i) and i == 0):
                        dve.wait_ge(turned, i * (HEADS * GROUPS) + ((h + 1) * GROUPS - HEADS * GROUPS))
                    wait_apart(dve, c, scored, i * (2 * HEADS) + (2 * h + half + 1))
                    cols = slice(half * HALF, (half + 1) * HALF)
                    nc.vector.tensor_tensor_reduce(
                        out=t[:, h, cols], in0=scores[:, cols], in1=mask[p][:, cols], scale=1.0, scalar=-3.0e38,
                        op0=ALU.add, op1=ALU.max, accum_out=part_max[:, h, half:half + 1]).then_inc(part_done, 1)

                def negate(i, h):
                    dve.wait_ge(part_done, i * (2 * HEADS) + (2 * h + 2))
                    nc.vector.tensor_scalar(neg_max[:, h:h + 1], part_max[:, h, 0:1], part_max[:, h, 1:2], -1.0,
                                            ALU.max, ALU.mult).then_inc(neg_max_done, 1)

                def copy_blocks(i, p, h, g):
                    dve.wait_ge(turned, i * (HEADS * GROUPS) + (h * GROUPS + g + 1))
                    nc.vector.tensor_copy(pt[p][:, h, g * BLOCKS:(g + 1) * BLOCKS, :].rearrange("p m n -> p (m n)"),
                                          blocks[:, (g % 2) * BANK:(g % 2 + 1) * BANK]).then_inc(pt_dve, 1)

                def divide(i):
                    dve.wait_ge(av_done, i * GROUPS + GROUPS)
                    dve.wait_ge(inv_t_done, i + 1)
                    if not (static(i) and i == 0):
                        dve.wait_ge(projected, i)
                    nc.vector.tensor_tensor(o_t[:], av[:, 0:P], inv_t[:], ALU.mult).then_inc(o_done, 1)

                def invert(i, p):
                    dve.wait_ge(prob_done, i * HEADS + HEADS)
                    nc.vector.reciprocal(inv_sum[:], row_sum[p][:]).then_inc(inv_done, 1)
                    dve.wait_ge(inv_done, i + 1)
                    if not (static(i) and i == 0):
                        dve.wait_ge(wide_turned, i)
                    nc.vector.tensor_copy(inv_wide[:], inv_sum[:].unsqueeze(2).broadcast_to([P, HEADS, HD])).then_inc(wide_done, 1)

                def add_residual(i, p):
                    dve.wait_ge(projected, i + 1)
                    dve.wait_ge(res_done, i + 1)
                    nc.vector.tensor_tensor(z[:], misc[:, P:2 * P], res[p][:], ALU.add).then_inc(z_done, 1)

                def moments(i):
                    dve.wait_ge(z_done, i + 1)
                    nc.vector.bn_stats(out=stats[:], in_=z[:]).then_inc(stats_done, 1)

                def gather_moments(i):
                    wait_apart(dve, c, stats_done, i + 1)
                    nc.vector.bn_aggr(out=mean_var[:], in_=stats[:]).then_inc(mv_done, 1)

                def add_eps(i):
                    dve.wait_ge(mv_done, i + 1)
                    nc.vector.tensor_scalar(var_eps[:], mean_var[:, 1:2], EPS, None, ALU.add).then_inc(eps_done, 1)

                def norm(i, p):
                    add_residual(i, p)
                    moments(i)
                    gather_moments(i)
                    add_eps(i)

                def finish_norm(i, p, n):
                    dve.wait_ge(rstd_done, i + 1)
                    if not (static(i) and i < 2):
                        dve.wait_ge(out_stored[p], 16 * (n - 1))
                    nc.vector.tensor_scalar(normed[p][:], z[:], mean_var[:, 0:1], rstd[:], ALU.subtract,
                                            ALU.mult).then_inc(normed_done, 1)

                def step(i, p, g):
                    for h in range(HEADS):
                        mine = [k for k in range(GROUPS) if COPIES[h][k] == "D"]
                        ahead = (i, p, h + 2, g + 1) if h < 2 else (i + 1, 1 - p, h - 2, g + 1 + p)
                        copy_blocks(i, p, h, mine[0])
                        if h == 0:
                            if not (static(i) and i < 2):
                                divide(i - 2)
                            if not (static(i) and i == 0):
                                invert(i - 1, 1 - p)
                        behind = not (static(i) and i < 2)
                        if behind and h == 2:
                            add_residual(i - 2, p)
                        if behind and h == 3:
                            gather_moments(i - 2)
                        more = not (static(i) and i == TILES - 1 and h >= 2)
                        if more:
                            masked(*ahead[:3], 0, ahead[3])
                        if behind and h == 2:
                            moments(i - 2)
                        if behind and h == 3:
                            add_eps(i - 2)
                        for k in mine[1:]:
                            copy_blocks(i, p, h, k)
                        if more:
                            masked(*ahead[:3], 1, ahead[3])
                            negate(ahead[0], ahead[2])
                        if behind and h == 3:
                            finish_norm(i - 2, p, g)

                for h in range(2):
                    for half in range(2):
                        masked(0, 0, h, half, 1)
                    negate(0, h)
                for i in range(4):
                    step(i, i % 2, i // 2)
                with dve.Fori(2, TILES // 2 - 1) as g:
                    for p in range(2):
                        step(g * 2 + p, p, g)
                step(TILES - 2, 0, TILES // 2 - 1)
                step(TILES - 1, 1, TILES // 2 - 1)
                divide(TILES - 2)
                invert(TILES - 1, 1)
                norm(TILES - 2, 0)
                finish_norm(TILES - 2, 0, TILES // 2)
                divide(TILES - 1)
                norm(TILES - 1, 1)
                finish_norm(TILES - 1, 1, TILES // 2)


def program(nc, io, out):
    with ExitStack() as hold:
        dram = scratch(nc)
        c = constants(nc, hold, io)
        layer0(nc, io, dram, c, 1, "l0")
        general = nc.values_load(c["general"][0:1, 0:1], min_val=0, max_val=1)
        with nc.If(general > 0):
            layer0(nc, io, dram, c, KINDS, "l0g")
        layer1(nc, dram, c, out)


def layout(inputs):
    import numpy as np
    f = {k: np.asarray(v) for k, v in inputs.items()}
    w = f["L1_gnn_in_proj_w"]
    bias = f["L1_gnn_in_proj_b"]
    return {
        "x": np.ascontiguousarray(f["x"]),
        "adj": np.ascontiguousarray(f["adj"]),
        "a": np.ascontiguousarray(np.stack([f[f"L0_gnn_a_{k}"] for k in range(KINDS)], axis=1)),
        "w_qkv": np.ascontiguousarray(w.T),
        "w_out": np.ascontiguousarray(f["L1_gnn_out_w"].T),
        "b_qk": np.ascontiguousarray(bias[:2 * D].reshape(2, D).T),
        "b_v": np.ascontiguousarray(np.broadcast_to(bias[2 * D:], (P, D))),
        "b_out": np.ascontiguousarray(np.broadcast_to(f["L1_gnn_out_b"], (P, D))),
    }


_SHAPES = ("x", "adj", "a", "w_qkv", "w_out", "b_qk", "b_v", "b_out")


def kernel(x, adj, L0_gnn_a_0, L0_gnn_a_1, L0_gnn_a_2, L0_gnn_a_3, L1_gnn_in_proj_w, L1_gnn_in_proj_b,
           L1_gnn_out_w, L1_gnn_out_b):
    import concourse.bacc as bacc
    from concourse.bass_utils import run_bass_kernel_spmd

    arrays = layout(dict(
        x=x, adj=adj, L0_gnn_a_0=L0_gnn_a_0, L0_gnn_a_1=L0_gnn_a_1, L0_gnn_a_2=L0_gnn_a_2, L0_gnn_a_3=L0_gnn_a_3,
        L1_gnn_in_proj_w=L1_gnn_in_proj_w, L1_gnn_in_proj_b=L1_gnn_in_proj_b, L1_gnn_out_w=L1_gnn_out_w,
        L1_gnn_out_b=L1_gnn_out_b))
    nc = bacc.Bacc("TRN2", target_bir_lowering=False, num_devices=1)
    io = {n: nc.dram_tensor(n, list(arrays[n].shape), mybir.dt.from_np(arrays[n].dtype), kind="ExternalInput").ap()
          for n in _SHAPES}
    out = nc.dram_tensor("out", [B, N, D], F32, kind="ExternalOutput").ap()
    program(nc, io, out)
    return run_bass_kernel_spmd(nc, [arrays], core_ids=[0]).results[0]["out"]
```
